# Optimizing a Trainium2 kernel written in Bass

```python
import numpy as np
import jax
import jax.numpy as jnp

def _softmax(x, axis=-1):
    return jax.nn.softmax(x, axis=axis)

def _gelu(x):
    return jax.nn.gelu(x, approximate=True)

def _silu(x):
    return jax.nn.silu(x)

def _sigmoid(x):
    return jax.nn.sigmoid(x)

def _layernorm(x, axis=-1, eps=1e-05):
    m = jnp.mean(x, axis=axis, keepdims=True)
    v = jnp.var(x, axis=axis, keepdims=True)
    return (x - m) / jnp.sqrt(v + eps)

def _scatter_add(tgt, idx, src, axis=0):
    return tgt.at[idx].add(src)

def _segment_sum(src, seg, n):
    return jax.ops.segment_sum(src, seg, n)
kernel_name = 'mk_cond_resid_d4_seqx_r2_3679d4'

def setup_inputs(seed: int=0):
    np.random.seed(seed)
    _w = jnp.asarray

    def _rec_inputs():
        import jax
        import jax.numpy as jnp
        _rk = jax.random.key(seed)
        x = 0.5 + 0.2887 * jax.random.normal(jax.random.fold_in(_rk, 1), (2, 2048, 512), jnp.float32)
        _lenS = 2048 - jax.random.randint(jax.random.fold_in(_rk, 7), (2,), 0, max(1, 2048 // 4) + 1, jnp.int32)
        _lenS2 = 2048 - jax.random.randint(jax.random.fold_in(_rk, 8), (2,), 0, max(1, 2048 // 4) + 1, jnp.int32)
        condB_zX = jax.random.uniform(jax.random.fold_in(_rk, 11), (2,), jnp.float32, 0.0, 0.983423)
        condB_zY = jax.random.uniform(jax.random.fold_in(_rk, 12), (2,), jnp.float32, 0.0, 0.979075)
        condB_zR = jax.random.uniform(jax.random.fold_in(_rk, 13), (2,), jnp.float32, 0.0, 0.9968)
        itok_B_0_3 = jax.random.randint(jax.random.fold_in(_rk, 14), (2,), 0, 4, jnp.int32)
        itok_B_0_30 = jax.random.randint(jax.random.fold_in(_rk, 15), (2,), 0, 31, jnp.int32)
        itok_B_0_2 = jax.random.randint(jax.random.fold_in(_rk, 16), (2,), 0, 3, jnp.int32)
        return (x, condB_zX, condB_zY, condB_zR, itok_B_0_3, itok_B_0_30, itok_B_0_2)
    x, condB_zX, condB_zY, condB_zR, itok_B_0_3, itok_B_0_30, itok_B_0_2 = _rec_inputs()

    def _L0_cond_setup():
        import jax, jax.numpy as jnp
        import numpy as np
        key = jax.random.key(seed)
        k1, k2, k3, k4 = jax.random.split(key, 4)
        B, H, W = (64, 512, 512)
        return {'y': jax.random.uniform(k1, (B, H, W), dtype=jnp.float32), 'zX': jax.random.uniform(k2, (B, 1), dtype=jnp.float32), 'zY': jax.random.uniform(k3, (B, 1), dtype=jnp.float32), 'zR': jax.random.uniform(k4, (B, 1), dtype=jnp.float32), 'dx': 1, 'dy': 1}
    _L0_cond_all = _L0_cond_setup()
    _L0_cond_in = {k: v for k, v in _L0_cond_all.items() if k in ()}
    del _L0_cond_all

    def _L1_cond_setup():
        import jax, jax.numpy as jnp
        import numpy as np
        D = 512
        RANK = 16
        ALPHA = 16.0
        SCALING = ALPHA / RANK
        N_LANG = 4
        B, S = (32, 1024)
        key = jax.random.key(seed)
        k1, k2, k3, k4, k5 = jax.random.split(key, 5)
        x = jax.random.normal(k1, (B, S, D), dtype=jnp.float32)
        language_ids = jax.random.randint(k2, (B,), 0, N_LANG, dtype=jnp.int32)
        lora_A = jax.random.normal(k3, (N_LANG, RANK, D), dtype=jnp.float32) * 0.02
        lora_B = jax.random.normal(k4, (N_LANG, D, RANK), dtype=jnp.float32) * 0.02
        lang_embed = jax.random.normal(k5, (N_LANG, D), dtype=jnp.float32) * 0.02
        return {'x': x, 'language_ids': language_ids, 'lora_A': lora_A, 'lora_B': lora_B, 'lang_embed': lang_embed}
    _L1_cond_all = _L1_cond_setup()
    _L1_cond_in = {k: v for k, v in _L1_cond_all.items() if k in ('lora_A', 'lora_B', 'lang_embed')}
    del _L1_cond_all

    def _L2_cond_setup():
        import jax, jax.numpy as jnp
        import numpy as np
        C, I, O = (32, 512, 512)
        B, T = (64, 256)
        key = jax.random.key(seed)
        kx, kc, kw, kb = jax.random.split(key, 4)
        x = jax.random.normal(kx, (B, T, I), dtype=jnp.float32)
        cat_ids = jax.random.randint(kc, (B,), 0, C)
        W = 0.02 * jax.random.normal(kw, (C, I, O), dtype=jnp.float32)
        b = jnp.zeros((C, O), dtype=jnp.float32)
        return {'x': x, 'cat_ids': cat_ids, 'W': W, 'b': b}
    _L2_cond_all = _L2_cond_setup()
    _L2_cond_in = {k: v for k, v in _L2_cond_all.items() if k in ('W', 'b')}
    del _L2_cond_all

    def _L3_cond_setup():
        import jax, jax.numpy as jnp
        import numpy as np
        NEG_INF = -1e+30
        key = jax.random.key(seed)
        k1, k2, k3, k4, k5 = jax.random.split(key, 5)
        B, S, D, A = (16, 512, 512, 128)
        hidden = jax.random.normal(k1, (B, S, D), dtype=jnp.float32)
        W1 = jax.random.normal(k2, (D, A), dtype=jnp.float32) / np.sqrt(D)
        b1 = jax.random.normal(k3, (A,), dtype=jnp.float32) * 0.01
        v = jax.random.normal(k4, (A,), dtype=jnp.float32) / np.sqrt(A)
        prompt_type_ids = jax.random.randint(k5, (B,), 0, 3, dtype=jnp.int32)
        return {'hidden': hidden, 'W1': W1, 'b1': b1, 'v': v, 'prompt_type_ids': prompt_type_ids}
    _L3_cond_all = _L3_cond_setup()
    _L3_cond_in = {k: v for k, v in _L3_cond_all.items() if k in ('W1', 'b1', 'v')}
    del _L3_cond_all
    return {'x': x, 'condB_zX': condB_zX, 'condB_zY': condB_zY, 'condB_zR': condB_zR, 'itok_B_0_3': itok_B_0_3, 'itok_B_0_30': itok_B_0_30, 'itok_B_0_2': itok_B_0_2, 'L1_cond_lora_A': _L1_cond_in['lora_A'], 'L1_cond_lora_B': _L1_cond_in['lora_B'], 'L1_cond_lang_embed': _L1_cond_in['lang_embed'], 'L2_cond_W': _L2_cond_in['W'], 'L2_cond_b': _L2_cond_in['b'], 'L3_cond_W1': _L3_cond_in['W1'], 'L3_cond_b1': _L3_cond_in['b1'], 'L3_cond_v': _L3_cond_in['v']}

def reference(x, condB_zX, condB_zY, condB_zR, itok_B_0_3, itok_B_0_30, itok_B_0_2, L1_cond_lora_A, L1_cond_lora_B, L1_cond_lang_embed, L2_cond_W, L2_cond_b, L3_cond_W1, L3_cond_b1, L3_cond_v):
    import jax
    import jax.numpy as jnp

    def _L0_cond_ref(y, zX, zY, zR, dx, dy):
        import jax, jax.numpy as jnp
        import numpy as np
        yp_x = jnp.pad(y, ((0, 0), (0, 0), (1, 1)), mode='reflect')
        lap_x = (yp_x[:, :, :-2] - 2.0 * y + yp_x[:, :, 2:]) / (dx * dx)
        yp_y = jnp.pad(y, ((0, 0), (1, 1), (0, 0)), mode='reflect')
        lap_y = (yp_y[:, :-2, :] - 2.0 * y + yp_y[:, 2:, :]) / (dy * dy)
        du_dt = zX[:, :, None] * lap_x + zY[:, :, None] * lap_y + zR[:, :, None] * y * (1.0 - y)
        return du_dt

    def _L1_cond_ref(x, language_ids, lora_A, lora_B, lang_embed):
        import jax, jax.numpy as jnp
        import numpy as np
        D = 512
        RANK = 16
        ALPHA = 16.0
        SCALING = ALPHA / RANK
        N_LANG = 4
        B, S = (32, 1024)
        A = lora_A[language_ids]
        Bm = lora_B[language_ids]
        emb = lang_embed[language_ids]
        t = jnp.einsum('bsd,brd->bsr', x, A)
        lora_out = jnp.einsum('bsr,bdr->bsd', t, Bm) * SCALING
        return lora_out + emb[:, None, :]

    def _L2_cond_ref(x, cat_ids, W, b):
        import jax, jax.numpy as jnp
        import numpy as np
        C, I, O = (32, 512, 512)
        B, T = (64, 256)
        selected_W = W[cat_ids]
        selected_b = b[cat_ids]
        if x.ndim == 2:
            return jnp.einsum('bi,bio->bo', x, selected_W) + selected_b
        return jnp.einsum('bti,bio->bto', x, selected_W) + selected_b[:, None, :]

    def _L3_cond_ref(hidden, W1, b1, v, prompt_type_ids):
        import jax, jax.numpy as jnp
        import numpy as np
        NEG_INF = -1e+30
        B, S, D = hidden.shape
        attn_in = jnp.tanh(jnp.einsum('bsd,da->bsa', hidden, W1) + b1)
        scores = jnp.einsum('bsa,a->bs', attn_in, v)
        idx = jnp.arange(S)
        j = idx[:, None]
        l = idx[None, :]
        prefix_m = l <= j
        postfix_m = l >= j
        cloze_m = l != j
        pt = prompt_type_ids[:, None, None]
        mask = jnp.where(pt == 0, prefix_m[None], jnp.where(pt == 1, postfix_m[None], cloze_m[None]))
        masked_scores = jnp.where(mask, scores[:, None, :], NEG_INF)
        p = jax.nn.softmax(masked_scores, axis=-1)
        cnt = jnp.sum(mask, axis=-1).astype(hidden.dtype)
        pooled = jnp.einsum('bjl,bld->bjd', p, hidden) / cnt[..., None]
        return pooled
    x = x + _L0_cond_ref(x, condB_zX[:, None], condB_zY[:, None], condB_zR[:, None], 1, 1)
    x = x + _L1_cond_ref(x, itok_B_0_3, L1_cond_lora_A, L1_cond_lora_B, L1_cond_lang_embed)
    x = x + _L2_cond_ref(x, itok_B_0_30, L2_cond_W, L2_cond_b)
    x = x + _L3_cond_ref(x, L3_cond_W1, L3_cond_b1, L3_cond_v, itok_B_0_2)
    return x

_drawn_inputs = setup_inputs


def setup_inputs(seed=0):
    import zlib

    import numpy as np

    out = dict(_drawn_inputs(seed))
    spreads = {'L2_cond_b': (0.0, 0.1)}
    factors = {}
    for name, (base, spread) in spreads.items():
        noise = np.random.default_rng([zlib.crc32(name.encode()), seed]).standard_normal(out[name].shape)
        drawn = base * np.exp(spread * noise) if base else spread * noise
        out[name] = jnp.asarray(drawn.astype(out[name].dtype))
    for name, factor in factors.items():
        out[name] = (out[name] * factor).astype(out[name].dtype)
    return out
```

```python
from contextlib import ExitStack

import numpy as np

import concourse.bass as bass
from concourse import mybir

F32 = mybir.dt.float32
F32R = mybir.dt.float32r
I32 = mybir.dt.int32
ALU = mybir.AluOpType
ACT = mybir.ActivationFunctionType
AX_X = mybir.AxisListType.X

P = 128
NEG = -1.0e30


def fused_layers(nc, x, z_x, z_y, z_r, lang_ids, cat_ids, prompt_ids, lora_a, lora_b, lang_embed,
                 cat_w, cat_b, w1, b1, v, out):
    BATCH, S, D = x.shape
    RANK = lora_a.shape[1]
    ATT = w1.shape[1]
    KC = D // P
    T = 4
    ROWS = P * T
    GROUPS = S // ROWS
    NG = BATCH * GROUPS
    NBLK = S // P
    NHALF = T // 2
    H2 = D // 2
    W2 = D - H2 + 2
    assert (KC, NBLK, RANK, ATT) == (4, 16, 16, P) and T == KC

    with ExitStack() as ctx:
        def sb(name, shape, dt=F32):
            return ctx.enter_context(nc.sbuf_tensor(name, shape, dt))

        def sem(name):
            return ctx.enter_context(nc.semaphore(name))

        x3 = sb("x3", [P, BATCH * NBLK, D])
        ident = sb("ident", [P, P])
        below = sb("below", [P, P])
        above = sb("above", [P, P])
        ones = sb("ones", [P, P])
        rep = sb("rep", [NBLK, P])
        sel_f = sb("sel_f", [P, P])
        sel_c = sb("sel_c", [P, P], F32R)
        row_no = sb("row_no", [P, NBLK], I32)
        row_nof = sb("row_nof", [P, NBLK])
        zs = sb("zs", [P, 3, BATCH])
        coef = sb("coef", [P, 3, BATCH])
        pid_i = sb("pid_i", [P, BATCH], I32)
        pidf = sb("pidf", [P, BATCH])
        kind = sb("kind", [P, 3, BATCH])
        pen = sb("pen", [P, 3, BATCH])
        cab = sb("cab", [P, 2, BATCH])
        count = sb("count", [P, BATCH, NBLK])
        mask = sb("mask", [P, BATCH, P])
        bm = sb("bm", [NBLK, BATCH, NBLK])
        bmt = sb("bmt", [NBLK, BATCH, NBLK])
        idx = sb("idx", [1, 2 * BATCH], I32)
        vec_rows = sb("vec_rows", [BATCH * KC + 2, P])
        vec = sb("vec", [P, BATCH * KC + 2])
        sc = sb("sc", [P, BATCH, NBLK])
        arena = (nc.sbuf_base + 63) // 64 * 64

        at = [arena]

        def sb_at(name, shape, dt=F32):
            t = nc.alloc_sbuf_tensor_at(name, shape, dt, offset=at[0])
            at[0] += (int(np.prod(shape[1:])) * 4 + 63) // 64 * 64
            return t

        y = [sb_at(f"y{i}", [P, T + 2, D + 2]) for i in range(2)]
        quad = [sb_at(f"quad{i}", [P, NHALF, D]) for i in range(2)]
        lap = sb_at("lap", [P, NHALF, D])
        x1 = [sb_at(f"x1_{i}", [P, NHALF, D]) for i in range(2)]
        xt_hi = [sb_at(f"xt_hi{i}", [P, KC, ROWS], F32R) for i in range(2)]
        xt_lo = [sb_at(f"xt_lo{i}", [P, KC, ROWS], F32R) for i in range(2)]
        g_hi = [sb_at(f"g_hi{b}", [P, KC, D], F32R) for b in range(BATCH)]
        g_lo = [sb_at(f"g_lo{b}", [P, KC, D], F32R) for b in range(BATCH)]
        gw_hi = [sb_at(f"gw_hi{b}", [P, KC, ATT], F32R) for b in range(BATCH)]
        gw_lo = [sb_at(f"gw_lo{b}", [P, KC, ATT], F32R) for b in range(BATCH)]
        w1_sb = sb_at("w1_sb", [P, KC, ATT])
        cbias = [sb_at(f"cbias{b}", [P, D]) for b in range(BATCH)]
        a_st = sb_at("a_st", [P, D], F32R)
        b_st = sb_at("b_st", [P, D], F32R)
        ct = sb_at("ct", [P, KC])
        pbias = sb_at("pbias", [P, BATCH])
        h_t = [sb_at(f"h_t{i}", [P, ROWS]) for i in range(2)]
        end1 = at[0]
        wg = x3[:, 24:24 + KC, :]
        gt = x3[:, 28:28 + KC, :]
        l1w = [x3[:, 22 + b, :].rearrange("p (c m) -> p c m", c=KC) for b in range(BATCH)]
        a_raw = [x3[:, 20 + b, :] for b in range(BATCH)]
        b_bc = [x3[:, 18 + b, :] for b in range(BATCH)]
        b_raw = [x3[:, 17, b * KC * RANK:(b + 1) * KC * RANK].rearrange("p (c r) -> p c r", c=KC)
                 for b in range(BATCH)]

        at[0] = arena
        xh = sb_at("xh", [P, NBLK, D + 2], F32R)
        xl = sb_at("xl", [P, NBLK, D + 2], F32R)
        pf = sb_at("pf", [P, NBLK, P])
        ph = sb_at("ph", [P, NBLK, P], F32R)
        pl = sb_at("pl", [P, NBLK, P], F32R)
        uf = sb_at("uf", [P, NBLK, P])
        us = sb_at("us", [P, NBLK, P], F32R)
        ew = sb_at("ew", [P, NBLK * P], F32R)
        cs = sb_at("cs", [P, D + 2], F32R)
        ot = [sb_at(f"ot{i}", [P, D]) for i in range(4)]
        selq = sb_at("selq", [NBLK, NBLK, P], F32R)
        s16 = sb_at("s16", [NBLK, P])
        pmx = sb_at("pmx", [NBLK, P + 1])
        sfx = sb_at("sfx", [NBLK, P + 1])
        mrow = sb_at("mrow", [NBLK, P])
        nmh = sb_at("nmh", [NBLK, P], F32R)
        nml = sb_at("nml", [NBLK, P], F32R)
        diagb = sb_at("diagb", [NBLK, NBLK])
        xb16 = sb_at("xb16", [NBLK, NBLK])
        tmp16 = sb_at("tmp16", [NBLK, NBLK])
        be = sb_at("be", [NBLK, 1])
        esub = sb_at("esub", [P, NBLK])
        e_f = sb_at("e_f", [P, NBLK])
        e_hi = sb_at("e_hi", [P, NBLK], F32R)
        e_lo = sb_at("e_lo", [P, NBLK], F32R)
        bmb = sb_at("bmb", [P, NBLK])
        zc = sb_at("zc", [P, NBLK])
        rz = sb_at("rz", [P, NBLK])
        assert max(at[0], end1) <= nc.sbuf_usable_end, (at[0], end1)

        out_ps = [ctx.enter_context(nc.psum_tensor(f"out_ps{i}", [P, 2, 512], F32)) for i in range(2)]
        sum_ps = ctx.enter_context(nc.psum_tensor("sum_ps", [P, 2, 512], F32))
        sc_ps = ctx.enter_context(nc.psum_tensor("sc_ps", [P, 512], F32))
        misc = ctx.enter_context(nc.psum_tensor("misc", [P, 512], F32))
        main_ps = [out_ps[0][:, 0, :], out_ps[0][:, 1, :], out_ps[1][:, 0, :]]
        pre_ps = out_ps[1][:, 1, :]
        tr_ps = [sum_ps[:, 0, :], sum_ps[:, 1, :]]
        nm_ps = [sc_ps, misc]

        idx_loaded = sem("idx_loaded")
        small_loaded = sem("small_loaded")
        w_loaded = [sem(f"w_loaded{b}") for b in range(BATCH)]
        y_loaded = [sem(f"y_loaded{i}") for i in range(2)]
        out_stored = [sem(f"out_stored{i}") for i in range(4)]
        pool_step = sem("pool_step")
        consts_made = sem("consts_made")
        zeroed = sem("zeroed")
        pads_made = sem("pads_made")
        dve_step = sem("dve_step")
        coef_made = sem("coef_made")
        vec_made = sem("vec_made")
        l0_step = sem("l0_step")
        lhs_built = sem("lhs_built")
        quad_made = sem("quad_made")
        transposed = sem("transposed")
        hi_made = sem("hi_made")
        lo_made = sem("lo_made")
        pre_made = sem("pre_made")
        tanh_made = sem("tanh_made")
        main_made = sem("main_made")
        x3_made = sem("x3_made")
        score_made = sem("score_made")
        piece_made = sem("piece_made")
        piece_hi = sem("piece_hi")
        piece_read = sem("piece_read")
        soft_pe = sem("soft_pe")
        soft_dve = sem("soft_dve")
        e_made = sem("e_made")
        ew_made = sem("ew_made")
        nm_made = sem("nm_made")
        arg_made = sem("arg_made")
        exp_made = sem("exp_made")
        wts_made = sem("wts_made")
        xh_made = sem("xh_made")
        xl_made = sem("xl_made")
        sums_made = sem("sums_made")
        cs_hi = sem("cs_hi")
        cs_made = sem("cs_made")
        pooled = sem("pooled")
        out_made = sem("out_made")

        N_SMALL = 7 + BATCH
        N_WLOAD = 7

        def y_loads(n):
            g = n % GROUPS
            return (3 if g == 0 else 1) + (3 if g == GROUPS - 1 else 1) + 1

        def y_count(n):
            return 16 * sum(y_loads(m) for m in range(n % 2, n + 1, 2))

        block = ctx.enter_context(nc.Block())

        @block.sync
        def _(sp):
            def load_group(n):
                b, g = divmod(n, GROUPS)
                r0 = g * ROWS
                t, s = y[n % 2], y_loaded[n % 2]
                if n >= 2:
                    sp.wait_ge(l0_step, 10 * (n - 1))
                sp.dma_start(t[:, 1:T + 1, 1:D + 1],
                             x[b, r0:r0 + ROWS, :].rearrange("(p t) d -> p t d", t=T)).then_inc(s, 16)
                if g == 0:
                    sp.dma_start(t[0:1, 0, 1:D + 1], x[b, 1:2, :]).then_inc(s, 16)
                    sp.dma_start(t[1:16, 0, 1:D + 1],
                                 x[b, T - 1:T - 1 + 15 * T, :].rearrange("(p t) d -> p t d", t=T)[:, 0, :]
                                 ).then_inc(s, 16)
                    sp.dma_start(t[16:P, 0, 1:D + 1],
                                 x[b, 16 * T - 1:ROWS - 1, :].rearrange("(p t) d -> p t d", t=T)[:, 0, :]
                                 ).then_inc(s, 16)
                else:
                    sp.dma_start(t[:, 0, 1:D + 1],
                                 x[b, r0 - 1:r0 - 1 + ROWS, :].rearrange("(p t) d -> p t d", t=T)[:, 0, :]
                                 ).then_inc(s, 16)
                if g == GROUPS - 1:
                    sp.dma_start(t[P - 1:P, T + 1, 1:D + 1], x[b, S - 2:S - 1, :]).then_inc(s, 16)
                    sp.dma_start(t[P - 16:P - 1, T + 1, 1:D + 1],
                                 x[b, S - 16 * T + T:S, :].rearrange("(p t) d -> p t d", t=T)[:, 0, :]
                                 ).then_inc(s, 16)
                    sp.dma_start(t[0:P - 16, T + 1, 1:D + 1],
                                 x[b, r0 + T:r0 + T + (P - 16) * T, :].rearrange("(p t) d -> p t d", t=T)[:, 0, :]
                                 ).then_inc(s, 16)
                else:
                    sp.dma_start(t[:, T + 1, 1:D + 1],
                                 x[b, r0 + T:r0 + T + ROWS, :].rearrange("(p t) d -> p t d", t=T)[:, 0, :]
                                 ).then_inc(s, 16)

            def load_weights(b):
                cat = sp.value_load(idx[0:1, b:b + 1], min_val=0, max_val=cat_w.shape[0] - 1)
                lang = sp.value_load(idx[0:1, BATCH + b:BATCH + b + 1], min_val=0, max_val=lora_a.shape[0] - 1)
                if b:
                    sp.wait_ge(piece_read, 13 * (b - 1) + 10)
                sp.dma_start(wg, cat_w[bass.ds(cat, 1)].rearrange("a (c p) o -> p (a c) o", p=P)
                             ).then_inc(w_loaded[b], 16)
                sp.dma_start(b_raw[b], lora_b[bass.ds(lang, 1)].rearrange("a (c p) r -> p (a c) r", p=P)
                             ).then_inc(w_loaded[b], 16)
                if b == 0:
                    sp.wait_ge(zeroed, 1)
                for i in range(4):
                    sp.dma_start(a_raw[b][32 * i:32 * i + RANK, :],
                                 lora_a[bass.ds(lang, 1)].rearrange("a r d -> (a r) d")
                                 ).then_inc(w_loaded[b], 16)
                sp.dma_start(b_bc[b], cat_b[bass.ds(cat, 1)].to_broadcast([P, D])).then_inc(w_loaded[b], 16)

            def load_embed(b):
                lang = sp.value_load(idx[0:1, BATCH + b:BATCH + b + 1], min_val=0, max_val=lora_a.shape[0] - 1)
                sp.dma_start(vec_rows[b * KC:(b + 1) * KC, :],
                             lang_embed[bass.ds(lang, 1)].rearrange("a (c p) -> (a c) p", p=P)
                             ).then_inc(small_loaded, 16)

            sp.dma_start(idx[0:1, 0:BATCH], cat_ids.rearrange("(a n) -> a n", a=1)).then_inc(idx_loaded, 16)
            sp.dma_start(idx[0:1, BATCH:2 * BATCH], lang_ids.rearrange("(a n) -> a n", a=1)).then_inc(idx_loaded, 16)
            load_group(0)
            sp.wait_ge(idx_loaded, 32)
            load_weights(0)
            for b in range(BATCH):
                load_embed(b)
            load_group(1)
            load_weights(1)
            for n in range(2, NG):
                load_group(n)

        @block.gpsimd
        def _(pool):
            steps = [0]

            def step(ins):
                steps[0] += 1
                ins.then_inc(pool_step, 1)

            step(pool.memset(ident[:], 0.0))
            step(pool.memset(below[:], 0.0))
            step(pool.memset(above[:], 0.0))
            step(pool.memset(sel_f[:], 0.0))
            step(pool.memset(rep[:], 0.0))
            pool.wait_ge(pool_step, steps[0])
            step(pool.affine_select(out=ident[:], in_=ident[:], compare_op=ALU.not_equal, fill=1.0,
                                    base=0, pattern=[[-1, P]], channel_multiplier=1))
            step(pool.affine_select(out=below[:], in_=below[:], compare_op=ALU.is_ge, fill=1.0,
                                    base=0, pattern=[[-1, P]], channel_multiplier=1))
            step(pool.affine_select(out=above[:], in_=above[:], compare_op=ALU.is_ge, fill=1.0,
                                    base=0, pattern=[[1, P]], channel_multiplier=-1))
            step(pool.affine_select(out=sel_f[:], in_=sel_f[:], compare_op=ALU.not_equal, fill=1.0,
                                    base=-RANK, pattern=[[0, P]], channel_multiplier=1))
            step(pool.affine_select(out=rep[:].rearrange("q (a m) -> q a m", m=NBLK),
                                    in_=rep[:].rearrange("q (a m) -> q a m", m=NBLK),
                                    compare_op=ALU.not_equal, fill=1.0,
                                    base=0, pattern=[[0, P // NBLK], [-1, NBLK]], channel_multiplier=1))
            step(pool.memset(ones[:], 1.0))
            step(pool.iota(row_no[:], [[P, NBLK]], base=1, channel_multiplier=1))
            pool.wait_ge(pool_step, steps[0])
            step(pool.affine_select(out=sel_f[:], in_=sel_f[:], compare_op=ALU.not_equal, fill=1.0,
                                    base=-(32 + RANK), pattern=[[0, P]], channel_multiplier=1))
            pool.wait_ge(pool_step, steps[0])
            pool.tensor_copy(row_nof[:], row_no[:]).then_inc(consts_made, 1)
            for n in range(NG):
                pool.wait_ge(y_loaded[n % 2], y_count(n))
                pool.tensor_copy(y[n % 2][:, 1:T + 1, 0:D + 2:D + 1],
                                 y[n % 2][:, 1:T + 1, 2:D:D - 3]).then_inc(pads_made, 1)

        @block.scalar
        def _(act):
            for dst, src in ((w1_sb[:], w1.rearrange("(c p) a -> p c a", p=P)),
                             (zs[:, 0, :], z_x.rearrange("(a n) -> a n", a=1).to_broadcast([P, BATCH])),
                             (zs[:, 1, :], z_y.rearrange("(a n) -> a n", a=1).to_broadcast([P, BATCH])),
                             (zs[:, 2, :], z_r.rearrange("(a n) -> a n", a=1).to_broadcast([P, BATCH])),
                             (pid_i[:], prompt_ids.rearrange("(a n) -> a n", a=1).to_broadcast([P, BATCH])),
                             (vec_rows[BATCH * KC:BATCH * KC + 1, :], b1.rearrange("(a n) -> a n", a=1)),
                             (vec_rows[BATCH * KC + 1:BATCH * KC + 2, :], v.rearrange("(a n) -> a n", a=1))):
                act.dma_start(dst, src).then_inc(small_loaded, 16)

            def make_quad(n, h):
                b = n // GROUPS
                if n == 0 and h == 0:
                    act.wait_ge(coef_made, 1)
                act.wait_ge(pads_made, n + 1)
                if n:
                    act.wait_ge(l0_step, 10 * (n - 1) + 5 * (h + 1))
                act.activation(quad[h][:], y[n % 2][:, 1 + NHALF * h:1 + NHALF * (h + 1), 1:D + 1],
                               ACT.Identity, bias=coef[:, 1, b:b + 1], scale=coef[:, 0, b:b + 1]
                               ).then_inc(quad_made, 1)

            def split_hi(n, c):
                act.wait_ge(transposed, KC * n + c + 1)
                if n >= 2:
                    act.wait_ge(main_made, T * (n - 1))
                act.activation(xt_hi[n % 2][:, c, :], tr_ps[c % 2], ACT.Copy).then_inc(hi_made, 1)

            def piece(b, i):
                if i == 0 or i == 11:
                    act.wait_ge(piece_made, 13 * b + i + 1)
                    if i == 0:
                        if b:
                            act.wait_ge(piece_read, 13 * (b - 1) + 6)
                        act.activation(b_st[:], misc[:], ACT.Copy).then_inc(piece_hi, 1)
                    else:
                        act.activation(gw_hi[b][:].rearrange("p c a -> p (c a)"), misc[:], ACT.Copy
                                       ).then_inc(piece_hi, 1)
                elif 2 <= i < 6:
                    act.wait_ge(piece_read, 13 * b + i + 1)
                    act.activation(g_hi[b][:, i - 2, :], wg[:, i - 2, :], ACT.Copy).then_inc(piece_hi, 1)

            def tanh(n):
                b = n // GROUPS
                act.wait_ge(pre_made, n + 1)
                act.wait_ge(piece_read, 13 * (b + 1))
                if n >= 2:
                    act.wait_ge(score_made, n - 1)
                act.activation(h_t[n % 2][:], pre_ps, ACT.Tanh, bias=pbias[:, b:b + 1]).then_inc(tanh_made, 1)

            for n in range(2):
                for h in range(2):
                    make_quad(n, h)
                if n == 0:
                    piece(0, 0)
                    for c in range(KC):
                        split_hi(0, c)
            for i in range(1, 13):
                piece(0, i)
            for n in range(NG):
                if n + 1 < NG:
                    for c in range(KC):
                        split_hi(n + 1, c)
                if n + 2 < NG:
                    for h in range(2):
                        make_quad(n + 2, h)
                tanh(n)
                if n < 4:
                    for i in PIECES[n]:
                        piece(1, i)

            for b in range(BATCH):
                for q in range(NBLK):
                    if b == 0 and q == 0:
                        act.wait_ge(score_made, NG)
                    if b:
                        act.wait_ge(pooled, NBLK * (b - 1) + q + 1)
                    act.activation(xh[:, q, 0:D], x3[:, b * NBLK + q, :], ACT.Copy).then_inc(xh_made, 1)
                    if q == 5:
                        act.wait_ge(soft_dve, 3 * b + 3)
                        act.activation(e_f[:], esub[:], ACT.Exp).then_inc(e_made, 1)
                for j in range(4):
                    c = slice(4 * j, 4 * j + 4)
                    act.wait_ge(arg_made, 4 * b + j + 1)
                    act.activation(pf[:, c, :], pf[:, c, :], ACT.Exp).then_inc(exp_made, 1)
                    act.activation(uf[:, c, :], uf[:, c, :], ACT.Exp).then_inc(exp_made, 1)
                    act.wait_ge(exp_made, 16 * b + 4 * j + 2)
                    act.activation(ph[:, c, :], pf[:, c, :], ACT.Copy).then_inc(exp_made, 1)
                    act.activation(us[:, c, :], uf[:, c, :], ACT.Copy).then_inc(exp_made, 1)
                act.wait_ge(sums_made, b + 1)
                act.activation(cs[:, 0:H2], sum_ps[:, 0, 0:H2], ACT.Copy).then_inc(cs_hi, 1)
                act.activation(cs[:, H2:D + 2], sum_ps[:, 1, 0:W2], ACT.Copy).then_inc(cs_hi, 1)

        @block.tensor
        def _(pe):
            def piece(b, i):
                k = 13 * b + i
                if k:
                    pe.wait_ge(piece_read, k)
                if i == 0:
                    pe.wait_ge(lhs_built, b + 1)
                    if b == 0:
                        pe.wait_ge(vec_made, 1)
                    for c in range(KC):
                        m = pe.matmul(misc[:], l1w[b][:, c, :], wg[:, c, :], start=(c == 0), stop=(c == KC - 1))
                elif i == 1:
                    m = pe.matmul(misc[:], sel_c[:], b_st[:], start=True, stop=True)
                elif i < 6:
                    c = i - 2
                    m = pe.matmul(misc[:], a_st[:, c * P:(c + 1) * P], b_st[:], start=True, stop=True)
                elif i < 10:
                    mc = i - 6
                    for c in range(KC):
                        m = pe.transpose(misc[:, c * P:(c + 1) * P], wg[:, c, mc * P:(mc + 1) * P], ident[:])
                elif i == 10:
                    for c in range(KC):
                        m = pe.matmul(misc[:, c:c + 1], cbias[b][0:1, c * P:(c + 1) * P], ones[0:1, 0:1],
                                      start=True, stop=True)
                elif i == 11:
                    for c in range(KC):
                        for mc in range(KC):
                            m = pe.matmul(misc[:, c * P:(c + 1) * P], gt[:, mc, c * P:(c + 1) * P],
                                          w1_sb[:, mc, :], start=(mc == 0), stop=(mc == KC - 1))
                else:
                    for mc in range(KC):
                        m = pe.matmul(misc[:, 0:1], w1_sb[:, mc, :], ct[:, mc:mc + 1],
                                      start=(mc == 0), stop=(mc == KC - 1))
                m.then_inc(piece_made, 1)

            def transpose_group(n):
                pe.wait_ge(l0_step, 10 * (n + 1))
                for c in range(KC):
                    k = KC * n + c
                    if k >= 2:
                        pe.wait_ge(lo_made, k - 1)
                    rows = tr_ps[c % 2].rearrange("d (p t) -> d t p", t=T)
                    for t in range(T):
                        m = pe.transpose(rows[:, t, :], x1[t // NHALF][:, t % NHALF, c * P:(c + 1) * P], ident[:])
                    m.then_inc(transposed, 1)

            def three(out, hi, lo, r_hi, r_lo, first, last):
                pe.matmul(out, hi, r_hi, start=first, stop=False)
                pe.matmul(out, hi, r_lo, start=False, stop=False)
                return pe.matmul(out, lo, r_hi, start=False, stop=last)

            def pre_group(n):
                b, i = n // GROUPS, n % 2
                pe.wait_ge(lo_made, KC * (n + 1))
                if n:
                    pe.wait_ge(tanh_made, n)
                for c in range(KC):
                    m = three(pre_ps, gw_hi[b][:, c, :], gw_lo[b][:, c, :], xt_hi[i][:, c, :], xt_lo[i][:, c, :],
                              c == 0, c == KC - 1)
                m.then_inc(pre_made, 1)

            def main_block(n, k):
                b, i, blk = n // GROUPS, n % 2, T * n + k
                if blk >= 3:
                    pe.wait_ge(x3_made, blk - 2)
                rows = slice(k * P, (k + 1) * P)
                for c in range(KC):
                    m = three(main_ps[blk % 3], xt_hi[i][:, c, rows], xt_lo[i][:, c, rows],
                              g_hi[b][:, c, :], g_lo[b][:, c, :], c == 0, c == KC - 1)
                m.then_inc(main_made, 1)

            def score_group(n):
                pe.wait_ge(tanh_made, n + 1)
                for k in range(T):
                    m = pe.matmul(sc_ps[:, T * n + k:T * n + k + 1], h_t[n % 2][:, k * P:(k + 1) * P],
                                  vec[:, BATCH * KC + 1:BATCH * KC + 2], start=True, stop=True)
                m.then_inc(score_made, 1)

            pe.wait_ge(consts_made, 1)
            pe.wait_ge(small_loaded, 16 * N_SMALL)
            pe.transpose(misc[:, 0:BATCH * KC + 2], vec_rows[:], ident[0:BATCH * KC + 2, 0:BATCH * KC + 2]
                         ).then_inc(soft_pe, 1)
            piece(0, 0)
            transpose_group(0)
            for i in range(1, 13):
                piece(0, i)
            for n in range(NG):
                if n + 1 < NG:
                    transpose_group(n + 1)
                if n == 0:
                    pe.wait_ge(piece_read, 13)
                if n == GROUPS:
                    pe.wait_ge(piece_read, 26)
                pre_group(n)
                todo = list(PIECES[n]) if n < 4 else []
                for k in range(T):
                    main_block(n, k)
                    if todo:
                        piece(1, todo.pop(0))
                while todo:
                    piece(1, todo.pop(0))
                score_group(n)

            for b in range(BATCH):
                pe.wait_ge(soft_dve, 3 * b + 1)
                pe.transpose(misc[0:NBLK, 0:P], sc[:, b, :], ident[:]).then_inc(soft_pe, 1)
                pe.wait_ge(soft_dve, 3 * b + 2)
                pe.matmul(misc[:, 0:NBLK], ones[0:NBLK, :], diagb[:], start=True, stop=True)
                pe.matmul(misc[:, NBLK:2 * NBLK], rep[:], xb16[:], start=True, stop=True).then_inc(soft_pe, 1)
                pe.wait_ge(soft_dve, 3 * b + 3)
                for j in range(4):
                    if j >= 2:
                        pe.wait_ge(arg_made, 4 * b + j - 1)
                    for k in range(4):
                        q = 4 * j + k
                        o = nm_ps[j % 2][:, k * P:(k + 1) * P]
                        pe.matmul(o, selq[:, q, :], nmh[:], start=True, stop=False)
                        m = pe.matmul(o, selq[:, q, :], nml[:], start=False, stop=True)
                    m.then_inc(nm_made, 1)
                pe.wait_ge(ew_made, b + 1)
                for q in range(NBLK):
                    pe.wait_ge(xl_made, NBLK * b + q + 1)
                    lhs = ew[:, q * P:(q + 1) * P]
                    for r, x_part in enumerate((xh, xl)):
                        st, en = q == 0 and r == 0, q == NBLK - 1 and r == 1
                        pe.matmul(sum_ps[:, 0, 0:H2], lhs, x_part[:, q, 0:H2], start=st, stop=en)
                        m = pe.matmul(sum_ps[:, 1, 0:W2], lhs, x_part[:, q, H2:D + 2], start=st, stop=en)
                m.then_inc(sums_made, 1)
                pe.wait_ge(wts_made, 2 * (4 * b + 4))
                for q in range(NBLK):
                    blk = NBLK * b + q
                    if blk >= 2:
                        pe.wait_ge(out_made, blk - 1)
                    o = out_ps[blk % 2]
                    for lhs, rhs, st in ((ph[:, q, :], xh, True), (ph[:, q, :], xl, False), (pl[:, q, :], xh, False)):
                        pe.matmul(o[:, 0, 0:H2], lhs, rhs[:, q, 0:H2], start=st, stop=False)
                        pe.matmul(o[:, 1, 0:W2], lhs, rhs[:, q, H2:D + 2], start=st, stop=False)
                    if q == 0:
                        pe.wait_ge(cs_made, b + 1)
                    pe.matmul(o[:, 0, 0:H2], us[:, q, :], cs[:, 0:H2], start=False, stop=True)
                    pe.matmul(o[:, 1, 0:W2], us[:, q, :], cs[:, H2:D + 2], start=False, stop=True
                              ).then_inc(pooled, 1)

        @block.vector
        def _(dve):
            chain = [0]

            def link(ins):
                chain[0] += 1
                ins.then_inc(dve_step, 1)
                dve.wait_ge(dve_step, chain[0])

            def setup():
                for b in range(BATCH):
                    link(dve.memset(l1w[b], 0.0))
                for b in range(BATCH):
                    m = dve.memset(a_raw[b], 0.0)
                    link(m)
                dve.engine_nop().then_inc(zeroed, 1)
                dve.wait_ge(consts_made, 1)
                dve.wait_ge(small_loaded, 16 * N_SMALL)
                link(dve.tensor_scalar(coef[:, 0, :], zs[:, 2, :], -1.0, None, ALU.mult))
                link(dve.tensor_tensor(coef[:, 2, :], zs[:, 0, :], zs[:, 1, :], ALU.add))
                link(dve.tensor_scalar(coef[:, 2, :], coef[:, 2, :], -2.0, 1.0, ALU.mult, ALU.add))
                dve.tensor_tensor(coef[:, 1, :], coef[:, 2, :], zs[:, 2, :], ALU.add).then_inc(coef_made, 1)

            def setup_masks():
                link(dve.tensor_copy(sel_c[:], sel_f[:]))
                link(dve.tensor_copy(pidf[:], pid_i[:]))
                link(dve.tensor_scalar(kind[:, 0, :], pidf[:], 0.0, None, ALU.is_equal))
                link(dve.tensor_scalar(kind[:, 1, :], pidf[:], 1.0, None, ALU.is_equal))
                link(dve.tensor_tensor(kind[:, 2, :], kind[:, 0, :], kind[:, 1, :], ALU.add))
                link(dve.tensor_scalar(kind[:, 2, :], kind[:, 2, :], -1.0, 1.0, ALU.mult, ALU.add))
                link(dve.tensor_scalar(pen[:, 0, :], kind[:, 1, :], NEG, None, ALU.mult))
                link(dve.tensor_scalar(pen[:, 1, :], kind[:, 2, :], NEG, None, ALU.mult))
                link(dve.tensor_scalar(pen[:, 2, :], kind[:, 0, :], NEG, None, ALU.mult))
                link(dve.tensor_tensor(cab[:, 0, :], kind[:, 0, :], kind[:, 1, :], ALU.subtract))
                link(dve.tensor_scalar(cab[:, 1, :], kind[:, 1, :], float(S + 1), None, ALU.mult))
                link(dve.scalar_tensor_tensor(cab[:, 1, :], kind[:, 2, :], float(S - 1), cab[:, 1, :],
                                              ALU.mult, ALU.add))
                for b in range(BATCH):
                    link(dve.tensor_scalar(count[:, b, :], row_nof[:], cab[:, 0, b:b + 1], cab[:, 1, b:b + 1],
                                           ALU.mult, ALU.add))
                    link(dve.tensor_scalar(mask[:, b, :], below[:], pen[:, 0, b:b + 1], None, ALU.mult))
                    link(dve.scalar_tensor_tensor(mask[:, b, :], ident[:], pen[:, 1, b:b + 1], mask[:, b, :],
                                                  ALU.mult, ALU.add))
                    link(dve.scalar_tensor_tensor(mask[:, b, :], above[:], pen[:, 2, b:b + 1], mask[:, b, :],
                                                  ALU.mult, ALU.add))
                    n = NBLK
                    for m, lo, hi in ((bm, 0, 2), (bmt, 2, 0)):
                        link(dve.tensor_scalar(m[:, b, :], below[0:n, 0:n], pen[0:n, lo, b:b + 1], None, ALU.mult))
                        link(dve.scalar_tensor_tensor(m[:, b, :], above[0:n, 0:n], pen[0:n, hi, b:b + 1], m[:, b, :],
                                                      ALU.mult, ALU.add))
                        link(dve.scalar_tensor_tensor(m[:, b, :], ident[0:n, 0:n], NEG, m[:, b, :],
                                                      ALU.mult, ALU.add))

            def build_lhs(b):
                dve.wait_ge(w_loaded[b], 16 * N_WLOAD)
                for i in range(4):
                    link(dve.tensor_copy(l1w[b][:, :, 32 * i:32 * i + RANK], b_raw[b]))
                for i in range(4):
                    link(dve.tensor_copy(l1w[b][:, :, 32 * i + RANK:32 * i + RANK + 1],
                                         vec[:, KC * b:KC * (b + 1)].rearrange("p (c o) -> p c o", o=1)))
                if b:
                    dve.wait_ge(piece_made, 13 * (b - 1) + 6)
                link(dve.tensor_copy(a_st[:], a_raw[b]))
                link(dve.tensor_tensor(a_st[64:P, :], a_raw[b][64:P, :], a_st[64:P, :].bitcast(F32), ALU.subtract))
                for c in range(KC):
                    d = wg[:, c, c * P:(c + 1) * P]
                    m = dve.tensor_tensor(d, d, ident[:], ALU.add)
                m.then_inc(lhs_built, 1)

            def piece(b, i):
                k = 13 * b + i
                dve.wait_ge(piece_made, k + 1)
                if i == 0:
                    dve.wait_ge(piece_hi, 6 * b + 1)
                    for s in (32, 96):
                        m = dve.tensor_tensor(b_st[s:s + 32, :], misc[s:s + 32, :], b_st[s:s + 32, :].bitcast(F32),
                                              ALU.subtract)
                elif i == 1:
                    m = dve.tensor_tensor(cbias[b][:], misc[:], b_bc[b], ALU.add)
                elif i < 6:
                    m = dve.tensor_tensor(wg[:, i - 2, :], misc[:], wg[:, i - 2, :], ALU.add)
                elif i < 10:
                    m = dve.tensor_copy(gt[:, i - 6, :], misc[:])
                elif i == 10:
                    m = dve.tensor_copy(ct[:], misc[:, 0:KC])
                elif i == 11:
                    dve.wait_ge(piece_hi, 6 * b + 6)
                    m = dve.tensor_tensor(gw_lo[b][:].rearrange("p c a -> p (c a)"), misc[:],
                                          gw_hi[b][:].rearrange("p c a -> p (c a)").bitcast(F32), ALU.subtract)
                else:
                    m = dve.tensor_tensor(pbias[:, b:b + 1], misc[:, 0:1], vec[:, BATCH * KC:BATCH * KC + 1], ALU.add)
                m.then_inc(piece_read, 1)
                if 2 <= i < 6:
                    dve.wait_ge(piece_hi, 6 * b + i)
                    link(dve.tensor_tensor(g_lo[b][:, i - 2, :], wg[:, i - 2, :], g_hi[b][:, i - 2, :].bitcast(F32),
                                           ALU.subtract))

            def stencil(n, h, o):
                b = n // GROUPS
                t = y[n % 2]
                r = 1 + NHALF * h
                k = 10 * n + 5 * h
                if o:
                    dve.wait_ge(l0_step, k + o)
                if o == 0:
                    if k:
                        dve.wait_ge(l0_step, k)
                    dve.wait_ge(pads_made, n + 1)
                    m = dve.tensor_tensor(lap[:], t[:, r:r + NHALF, 0:D], t[:, r:r + NHALF, 2:D + 2], ALU.add)
                elif o == 1:
                    dve.wait_ge(quad_made, 2 * n + h + 1)
                    m = dve.tensor_tensor(quad[h][:], quad[h][:], t[:, r:r + NHALF, 1:D + 1], ALU.mult)
                elif o == 2:
                    m = dve.scalar_tensor_tensor(lap[:], lap[:], zs[:, 0, b:b + 1], quad[h][:], ALU.mult, ALU.add)
                elif o == 3:
                    m = dve.tensor_tensor(quad[h][:], t[:, r - 1:r - 1 + NHALF, 1:D + 1],
                                          t[:, r + 1:r + 1 + NHALF, 1:D + 1], ALU.add)
                else:
                    if n:
                        dve.wait_ge(transposed, KC * n)
                    m = dve.scalar_tensor_tensor(x1[h][:], quad[h][:], zs[:, 1, b:b + 1], lap[:], ALU.mult, ALU.add)
                m.then_inc(l0_step, 1)

            def split_lo(n, c):
                dve.wait_ge(hi_made, KC * n + c + 1)
                if n >= 2:
                    dve.wait_ge(main_made, T * (n - 1))
                dve.tensor_tensor(xt_lo[n % 2][:, c, :], tr_ps[c % 2], xt_hi[n % 2][:, c, :].bitcast(F32),
                                  ALU.subtract).then_inc(lo_made, 1)

            def take_block(n, k):
                blk = T * n + k
                dve.wait_ge(main_made, blk + 1)
                dve.tensor_tensor(x3[:, blk, :], main_ps[blk % 3], cbias[n // GROUPS][:], ALU.add
                                  ).then_inc(x3_made, 1)

            setup()
            dve.wait_ge(soft_pe, 1)
            dve.tensor_copy(vec[:], misc[:, 0:BATCH * KC + 2]).then_inc(vec_made, 1)
            dve.wait_ge(vec_made, 1)
            build_lhs(0)
            for h in range(2):
                for o in range(5):
                    stencil(0, h, o)
            setup_masks()
            piece(0, 0)
            for c in range(KC):
                split_lo(0, c)
            todo = [(h, o) for h in range(2) for o in range(5)]
            for i in range(1, 13):
                piece(0, i)
                if todo:
                    stencil(1, *todo.pop(0))
            for n in range(NG):
                if n + 1 < NG:
                    for c in range(KC):
                        split_lo(n + 1, c)
                ops = [(h, o) for h in range(2) for o in range(5)] if n + 2 < NG else []
                todo = list(PIECES[n]) if n < 4 else []
                if n == 0:
                    build_lhs(1)
                for k in range(T):
                    for _ in range(3 if k % 2 == 0 else 2):
                        if ops:
                            stencil(n + 2, *ops.pop(0))
                    take_block(n, k)
                    if todo:
                        piece(1, todo.pop(0))
                while todo:
                    piece(1, todo.pop(0))

            dve.wait_ge(score_made, NG)
            link(dve.memset(ew[:].bitcast(F32), 0.0))
            link(dve.tensor_copy(selq[:], ident[0:NBLK, 0:NBLK].rearrange("k (q o) -> k q o", o=1)
                                 .to_broadcast([NBLK, NBLK, P])))
            link(dve.memset(xh[:, :, D:D + 2].bitcast(F32), 1.0))
            link(dve.memset(xl[:, :, D:D + 2].bitcast(F32), 0.0))
            link(dve.memset(pmx[:, 0:1], NEG))
            link(dve.memset(sfx[:, P:P + 1], NEG))
            link(dve.tensor_copy(sc[:].rearrange("p b q -> p (b q)"), sc_ps[:, 0:BATCH * NBLK]))
            for b in range(BATCH):
                dve.engine_nop().then_inc(soft_dve, 1)
                dve.wait_ge(soft_pe, 2 * b + 2)
                link(dve.tensor_copy(s16[:], misc[0:NBLK, 0:P]))
                link(dve.tensor_tensor_scan(pmx[:, 1:P + 1], s16[:], s16[:], NEG, ALU.max, ALU.max))
                link(dve.tensor_tensor_scan(sfx[:, P - 1::-1], s16[:, P - 1::-1], s16[:, P - 1::-1], NEG,
                                            ALU.max, ALU.max))
                if b:
                    dve.wait_ge(soft_pe, 2 * b + 1)
                link(dve.tensor_scalar(diagb[:], ident[0:NBLK, 0:NBLK], pmx[:, P:P + 1], None, ALU.mult))
                dve.tensor_scalar(xb16[:], bm[:, b, :], pmx[:, P:P + 1], None, ALU.add).then_inc(soft_dve, 1)
                dve.wait_ge(soft_pe, 2 * b + 3)
                link(dve.tensor_tensor(esub[:], sc[:, b, :], misc[:, 0:NBLK], ALU.subtract))
                link(dve.tensor_copy(bmb[:], misc[:, NBLK:2 * NBLK]))
                link(dve.tensor_tensor(tmp16[:], misc[0:NBLK, 0:NBLK], bmt[:, b, :], ALU.add))
                link(dve.reduce_max(be[:], tmp16[:], AX_X))
                link(dve.tensor_scalar(mrow[:], pmx[:, 0:P], pen[0:NBLK, 0, b:b + 1], be[:], ALU.add, ALU.max))
                link(dve.scalar_tensor_tensor(mrow[:], sfx[:, 1:P + 1], pen[0:NBLK, 2, b:b + 1], mrow[:],
                                              ALU.add, ALU.max))
                link(dve.scalar_tensor_tensor(mrow[:], s16[:], pen[0:NBLK, 1, b:b + 1], mrow[:], ALU.add, ALU.max))
                if b:
                    dve.wait_ge(nm_made, 4 * b)
                link(dve.tensor_scalar(nmh[:], mrow[:], -1.0, None, ALU.mult))
                dve.scalar_tensor_tensor(nml[:], mrow[:], -1.0, nmh[:].bitcast(F32), ALU.mult, ALU.subtract
                                         ).then_inc(soft_dve, 1)
                dve.wait_ge(e_made, b + 1)
                link(dve.tensor_copy(e_hi[:], e_f[:]))
                link(dve.tensor_tensor(e_lo[:], e_f[:], e_hi[:].bitcast(F32), ALU.subtract))
                if b:
                    dve.wait_ge(sums_made, b)
                for i in range(4):
                    link(dve.tensor_copy(ew[:, 32 * i::P + 1], e_hi[:].bitcast(F32)))
                    m = dve.tensor_copy(ew[:, 32 * i + NBLK::P + 1], e_lo[:].bitcast(F32))
                    if i < 3:
                        link(m)
                m.then_inc(ew_made, 1)

                def low_part(q):
                    dve.wait_ge(xh_made, NBLK * b + q + 1)
                    dve.tensor_tensor(xl[:, q, 0:D], x3[:, b * NBLK + q, :], xh[:, q, 0:D].bitcast(F32),
                                      ALU.subtract).then_inc(xl_made, 1)

                for j in range(4):
                    c = slice(4 * j, 4 * j + 4)
                    dve.wait_ge(nm_made, 4 * b + j + 1)
                    if b and j == 0:
                        dve.wait_ge(pooled, NBLK * b)
                    for k in range(4):
                        dve.scalar_tensor_tensor(pf[:, 4 * j + k, :], nm_ps[j % 2][:, k * P:(k + 1) * P],
                                                 sc[:, b, 4 * j + k:4 * j + k + 1], mask[:, b, :], ALU.add, ALU.add)
                    dve.tensor_tensor(uf[:, c, :], nm_ps[j % 2][:].rearrange("p (q i) -> p q i", q=4),
                                      bmb[:, c].rearrange("p (q o) -> p q o", o=1).to_broadcast([P, 4, P]),
                                      ALU.add).then_inc(arg_made, 1)
                    for q in range(4 * j, 4 * j + 4):
                        low_part(q)
                for j in range(4):
                    c = slice(4 * j, 4 * j + 4)
                    dve.wait_ge(exp_made, 16 * b + 4 * j + 4)
                    dve.tensor_tensor(pl[:, c, :], pf[:, c, :], ph[:, c, :].bitcast(F32), ALU.subtract
                                      ).then_inc(wts_made, 1)
                    dve.tensor_tensor(us[64:P, c, :], uf[64:P, c, :], us[64:P, c, :].bitcast(F32), ALU.subtract
                                      ).then_inc(wts_made, 1)
                dve.wait_ge(cs_hi, 2 * b + 2)
                for s in (32, 96):
                    for half, lo, n in ((0, 0, H2), (1, H2, W2)):
                        m = dve.tensor_tensor(cs[s:s + 32, lo:lo + n], sum_ps[s:s + 32, half, 0:n],
                                              cs[s:s + 32, lo:lo + n].bitcast(F32), ALU.subtract)
                m.then_inc(cs_made, 1)
                for q in range(NBLK):
                    blk = NBLK * b + q
                    dve.wait_ge(pooled, blk + 1)
                    o = out_ps[blk % 2]
                    link(dve.tensor_tensor(zc[:, q:q + 1], o[:, 1, D - H2:D - H2 + 1], count[:, b, q:q + 1], ALU.mult))
                    link(dve.reciprocal(rz[:, q:q + 1], zc[:, q:q + 1]))
                    if blk >= 4:
                        dve.wait_ge(out_stored[blk % 4], 16 * (blk // 4))
                    dve.scalar_tensor_tensor(ot[blk % 4][:].rearrange("p (a d) -> p a d", a=2), o[:, :, 0:H2],
                                             rz[:, q:q + 1],
                                             x3[:, blk, :].rearrange("p (a d) -> p a d", a=2), ALU.mult, ALU.add
                                             ).then_inc(out_made, 1)

        @block.sync
        def _(sp):
            for blk in range(BATCH * NBLK):
                b, q = divmod(blk, NBLK)
                sp.wait_ge(out_made, blk + 1)
                sp.dma_start(out[b, q * P:(q + 1) * P, :], ot[blk % 4][:]).then_inc(out_stored[blk % 4], 16)
            for i in range(4):
                sp.wait_ge(out_stored[i], 16 * (BATCH * NBLK // 4))


PIECES = [(0, 1), (2, 3, 4, 5), (6, 7, 8, 9), (10, 11, 12)]

_INS = ["x", "condB_zX", "condB_zY", "condB_zR", "itok_B_0_3", "itok_B_0_30", "itok_B_0_2", "L1_cond_lora_A",
        "L1_cond_lora_B", "L1_cond_lang_embed", "L2_cond_W", "L2_cond_b", "L3_cond_W1", "L3_cond_b1", "L3_cond_v"]


def kernel(**inputs):
    import concourse.bacc as bacc
    from concourse.bass_utils import run_bass_kernel_spmd

    nc = bacc.Bacc("TRN2", target_bir_lowering=False, num_devices=1)
    arrays, args = {}, []
    for name in _INS:
        a = np.ascontiguousarray(inputs[name])
        arrays[f"in_{name}"] = a
        args.append(nc.dram_tensor(f"in_{name}", a.shape, mybir.dt.from_np(a.dtype), kind="ExternalInput").ap())
    shape = tuple(inputs["x"].shape)
    args.append(nc.dram_tensor("out", shape, F32, kind="ExternalOutput").ap())
    fused_layers(nc, *args)
    r = run_bass_kernel_spmd(nc, [arrays], core_ids=[0])
    return r.results[0]["out"]
```

```python
from contextlib import ExitStack

import numpy as np

import concourse.bass as bass
from concourse import mybir

F32 = mybir.dt.float32
F32R = mybir.dt.float32r
I32 = mybir.dt.int32
ALU = mybir.AluOpType
ACT = mybir.ActivationFunctionType
AX_X = mybir.AxisListType.X

P = 128
NEG = -1.0e30


def fused_layers(nc, x, z_x, z_y, z_r, lang_ids, cat_ids, prompt_ids, lora_a, lora_b, lang_embed,
                 cat_w, cat_b, w1, b1, v, out):
    BATCH, S, D = x.shape
    RANK = lora_a.shape[1]
    ATT = w1.shape[1]
    KC = D // P
    T = 4
    ROWS = P * T
    GROUPS = S // ROWS
    NG = BATCH * GROUPS
    NBLK = S // P
    NHALF = T // 2
    assert (KC, NBLK, RANK, ATT) == (4, 16, 16, P) and T == KC

    with ExitStack() as ctx:
        def sb(name, shape, dt=F32):
            return ctx.enter_context(nc.sbuf_tensor(name, shape, dt))

        def sem(name):
            return ctx.enter_context(nc.semaphore(name))

        x3 = sb("x3", [P, BATCH * NBLK, D])
        ident = sb("ident", [P, P])
        pick = sb("pick", [32 + NBLK, NBLK], F32R)
        ones = sb("ones", [P, P])
        rep = sb("rep", [NBLK, P])
        sel = sb("sel", [P, 2, P], F32R)
        row_no = sb("row_no", [P, NBLK], I32)
        row_nof = sb("row_nof", [P, NBLK])
        zs = sb("zs", [P, 3, BATCH])
        coef = sb("coef", [P, 2, BATCH])
        pid_i = sb("pid_i", [P, BATCH], I32)
        pidf = sb("pidf", [P, BATCH])
        kind = sb("kind", [P, 3, BATCH])
        pen = sb("pen", [P, 3, BATCH])
        z_sum = sb("z_sum", [P, BATCH])
        count_ab = sb("count_ab", [P, 3, BATCH])
        count = sb("count", [P, BATCH, NBLK])
        mask = sb("mask", [P, BATCH, P])
        bm = sb("bm", [NBLK, BATCH, NBLK])
        bmt = sb("bmt", [NBLK, BATCH, NBLK])
        idx = sb("idx", [1, 2 * BATCH], I32)
        vec = sb("vec", [P, BATCH * KC + 2])
        sc = sb("sc", [P, BATCH, NBLK])
        diagb = sb("diagb", [NBLK, NBLK])
        xb16 = sb("xb16", [NBLK, NBLK])
        tmp16 = sb("tmp16", [NBLK, NBLK])
        be = sb("be", [NBLK, 1])
        e_quad = sb("e_quad", [P, P])
        zb = sb("zb", [P, BATCH, 2], F32R)
        ones_r = sb("ones_r", [P, 2], F32R)
        esub = sb("esub", [P, NBLK])
        e_f = sb("e_f", [P, NBLK])
        e_hi = sb("e_hi", [P, NBLK], F32R)
        e_lo = sb("e_lo", [P, NBLK], F32R)
        bmb = sb("bmb", [P, NBLK])
        zc = sb("zc", [P, NBLK])
        rz = sb("rz", [P, BATCH, NBLK])
        ew = sb("ew", [P, NBLK * P], F32R)
        ph0 = sb("ph0", [P, NBLK, P], F32R)
        pl0 = sb("pl0", [P, NBLK, P], F32R)

        at = [(nc.sbuf_base + 63) // 64 * 64]

        def sb_at(name, shape, dt=F32):
            where = at[0]
            t = nc.alloc_sbuf_tensor_at(name, shape, dt, offset=where)
            at[0] += (int(np.prod(shape[1:])) * 4 + 63) // 64 * 64
            return t, where

        def over(name, shape, dt, where, end):
            assert where + int(np.prod(shape[1:])) * 4 <= end
            return nc.alloc_sbuf_tensor_at(name, shape, dt, offset=where)

        (y0, y_at), (y1, _) = [sb_at(f"y{i}", [P, T + 2, D + 2]) for i in range(2)]
        y = [y0, y1]
        quad = [sb_at(f"quad{i}", [P, NHALF, D])[0] for i in range(2)]
        lap, _ = sb_at("lap", [P, NHALF, D])
        (x1a, x1_at), (x1b, _) = [sb_at(f"x1_{i}", [P, NHALF, D]) for i in range(2)]
        x1 = [x1a, x1b]
        (xh0, xt0_at), (xl0, _) = sb_at("xt_hi0", [P, KC, ROWS], F32R), sb_at("xt_lo0", [P, KC, ROWS], F32R)
        (xh1, xt1_at), (xl1, _) = sb_at("xt_hi1", [P, KC, ROWS], F32R), sb_at("xt_lo1", [P, KC, ROWS], F32R)
        xt_hi, xt_lo = [xh0, xh1], [xl0, xl1]
        xt_end = at[0]
        g_hi, g_lo, gw_hi, gw_lo, g_at = [], [], [], [], []
        for b in range(BATCH):
            g_at.append(at[0])
            g_hi.append(sb_at(f"g_hi{b}", [P, KC, D], F32R)[0])
            g_lo.append(sb_at(f"g_lo{b}", [P, KC, D], F32R)[0])
            gw_hi.append(sb_at(f"gw_hi{b}", [P, KC, ATT], F32R)[0])
            gw_lo.append(sb_at(f"gw_lo{b}", [P, KC, ATT], F32R)[0])
        a_st, _ = sb_at("a_st", [P, D], F32R)
        b_st, _ = sb_at("b_st", [P, D], F32R)
        g_end = at[0]
        w1_sb, _ = sb_at("w1_sb", [P, KC, ATT])
        c_st = [sb_at(f"c_st{b}", [64, D], F32R)[0] for b in range(BATCH)]
        ct, _ = sb_at("ct", [P, KC])
        pbias, _ = sb_at("pbias", [P, BATCH])
        h_t, _ = sb_at("h_t", [P, ROWS])
        assert at[0] <= nc.sbuf_usable_end, at[0] - nc.sbuf_usable_end
        wg = x3[:, 24:24 + KC, :]
        gt = x3[:, 28:28 + KC, :]
        l1w = [x3[:, 22 + b, :].rearrange("p (c m) -> p c m", c=KC) for b in range(BATCH)]
        a_raw = [x3[:, 20 + b, :] for b in range(BATCH)]
        b_bc = [x3[:, 18 + b, :] for b in range(BATCH)]
        b_raw = [x3[:, 17, b * KC * RANK:(b + 1) * KC * RANK].rearrange("p (c r) -> p c r", c=KC)
                 for b in range(BATCH)]
        vec_rows = x3[0:BATCH * KC + 2, 17, 128:256]
        pool_tmp = x3[:, 17, 256:384]
        below, above = x3[:, 16, 0:P], x3[:, 16, P:2 * P]
        sel_f = x3[:, 16, 2 * P:4 * P].rearrange("p (i m) -> p i m", i=2)
        cbias = [x3[:, 14 + b, :] for b in range(BATCH)]

        row = D * 4
        xh = over("xh", [P, NBLK, D], F32R, y_at, x1_at)
        xl_x1 = over("xl_x1", [P, 4, D], F32R, x1_at, xt0_at)
        xl_t0 = over("xl_t0", [P, 8, D], F32R, xt0_at, xt1_at)
        xl_t1 = over("xl_t1", [P, 4, D], F32R, xt1_at, xt_end)
        xl = [(xl_x1, q) if q < 4 else (xl_t0, q - 4) if q < 12 else (xl_t1, q - 12) for q in range(NBLK)]
        xl = [t[:, i, :] for t, i in xl]
        ot_all = over("ot", [P, 4, D], F32, xt1_at + 4 * row, xt_end)
        ot = [ot_all[:, i, :] for i in range(4)]
        spare = y_at + NBLK * row
        small = []
        for name, w, dt in (("s16", P, F32), ("pmx", P + 1, F32), ("sfx", P + 1, F32), ("mrow", P, F32),
                            ("nm_st", P, F32R)):
            small.append(over(name, [32 + NBLK if name == "nm_st" else NBLK, w], dt, spare, x1_at))
            spare += (w * 4 + 31) // 32 * 32
        s16, pmx, sfx, mrow, nm_st = small
        cs = over("cs", [P, D], F32R, g_at[0] + 8 * row, g_at[1])
        us0 = over("us0", [P, NBLK, P], F32R, g_at[0], g_at[1])
        pu = over("pu", [P, 2, 2, 4, P], F32, g_at[0] + 4 * row, g_at[0] + 8 * row)
        ph1 = over("ph1", [P, NBLK, P], F32R, g_at[1], g_end)
        pl1 = over("pl1", [P, NBLK, P], F32R, g_at[1] + 4 * row, g_end)
        us1 = over("us1", [P, NBLK, P], F32R, g_at[1] + 8 * row, g_end)
        ph, pl, us = [ph0, ph1], [pl0, pl1], [us0, us1]

        banks = [ctx.enter_context(nc.psum_tensor(f"bank{i}", [P, 512], F32)) for i in range(8)]
        main_ps, pre_ps, tr_ps, sc_ps, misc = banks[0:3], banks[3], banks[4:6], banks[6], banks[7]
        nm_ps = [misc, tr_ps[1]]
        z_ps = tr_ps[0]
        sum_ps = pre_ps

        def piece_bank(b, i):
            if b:
                return misc
            return [misc, main_ps[1], main_ps[2], sc_ps][i % 4] if i < 6 else [misc, sc_ps][i % 2]

        idx_loaded = sem("idx_loaded")
        zs_loaded = sem("zs_loaded")
        vec_loaded = sem("vec_loaded")
        small_loaded = sem("small_loaded")
        w_loaded = [sem(f"w_loaded{b}") for b in range(BATCH)]
        y_loaded = [sem(f"y_loaded{i}") for i in range(2)]
        out_stored = [sem(f"out_stored{i}") for i in range(4)]
        pool_step = sem("pool_step")
        zeroed = sem("zeroed")
        consts_made = sem("consts_made")
        masks_made = sem("masks_made")
        pads_made = sem("pads_made")
        dve_step = sem("dve_step")
        coef_made = sem("coef_made")
        vec_rows_turned = sem("vec_rows_turned")
        vec_made = sem("vec_made")
        l0_step = sem("l0_step")
        act_step = sem("act_step")
        lhs_cols = sem("lhs_cols")
        lhs_built = sem("lhs_built")
        quad_made = sem("quad_made")
        transposed = sem("transposed")
        hi_made = sem("hi_made")
        lo_made = sem("lo_made")
        pre_made = sem("pre_made")
        tanh_made = sem("tanh_made")
        main_made = sem("main_made")
        x3_made = sem("x3_made")
        score_made = sem("score_made")
        piece_made = sem("piece_made")
        piece_hi = sem("piece_hi")
        piece_dve = sem("piece_dve")
        piece_act = sem("piece_act")
        g_split = sem("g_split")
        soft_pe = sem("soft_pe")
        soft_dve = sem("soft_dve")
        e_made = sem("e_made")
        e_split = sem("e_split")
        ew_made = sem("ew_made")
        nm_made = sem("nm_made")
        arg_made = sem("arg_made")
        exp_made = sem("exp_made")
        e_spread = sem("e_spread")
        zb_hi = sem("zb_hi")
        zb_made = sem("zb_made")
        z_made = sem("z_made")
        rz_made = sem("rz_made")
        wt_hi = sem("wt_hi")
        wt_lo = sem("wt_lo")
        xh_made = sem("xh_made")
        xl_dve = sem("xl_dve")
        xl_pool = sem("xl_pool")
        sums_made = sem("sums_made")
        cs_hi = sem("cs_hi")
        cs_made = sem("cs_made")
        pooled = sem("pooled")
        out_act = sem("out_act")
        out_dve = sem("out_dve")
        out_pool = sem("out_pool")

        N_VEC = BATCH + 2
        N_WLOAD = 7
        PIECES = 13
        BY_ACT = (6, 7, 8, 9, 10, 12)

        def count_of(mine, upto):
            return sum(1 for m in range(upto + 1) if mine(m))

        def read_by_act(k):
            return k % PIECES in BY_ACT

        def wait_piece_read(eng, k):
            if read_by_act(k):
                eng.wait_ge(piece_act, count_of(read_by_act, k))
            else:
                eng.wait_ge(piece_dve, count_of(lambda m: not read_by_act(m), k))

        def wait_x3(eng, blk):
            eng.wait_ge(x3_made, blk + 1)

        def low_by_pool(blk):
            return blk in POOL_LOWS

        def wait_low(eng, blk):
            if low_by_pool(blk):
                eng.wait_ge(xl_pool, count_of(low_by_pool, blk))
            else:
                eng.wait_ge(xl_dve, count_of(lambda m: not low_by_pool(m), blk))

        def shared_end(blk):
            return blk in SHARED_ENDS

        def wait_bank_taken(eng, blk):
            if shared_end(blk):
                eng.wait_ge(out_act, count_of(shared_end, blk))
            else:
                eng.wait_ge(out_dve, count_of(lambda m: not shared_end(m), blk))

        def wait_out(eng, blk):
            if shared_end(blk):
                eng.wait_ge(out_pool, count_of(shared_end, blk))
            else:
                eng.wait_ge(out_dve, count_of(lambda m: not shared_end(m), blk))

        def y_loads(n):
            g = n % GROUPS
            return (3 if g == 0 else 1) + (3 if g == GROUPS - 1 else 1) + 1

        def y_count(n):
            return 16 * sum(y_loads(m) for m in range(n % 2, n + 1, 2))

        def wait_low_buffer(eng, blk):
            b, q = divmod(blk, NBLK)
            if b:
                eng.wait_ge(pooled, NBLK * (b - 1) + q + 1)
            elif q < 4:
                eng.wait_ge(transposed, KC * NG)
            elif q < 12:
                eng.wait_ge(main_made, T * (NG - 1))
            else:
                eng.wait_ge(main_made, T * NG)

        def low_part(eng, blk):
            q = blk % NBLK
            wait_low_buffer(eng, blk)
            eng.wait_ge(xh_made, blk + 1)
            return eng.tensor_tensor(xl[q], x3[:, blk, :], xh[:, q, :].bitcast(F32), ALU.subtract)

        def turn_at(n):
            return {2: (0, 1), 3: (2, 3)} if n == 0 else {0: (0, 1), 1: (2, 3)}

        block = ctx.enter_context(nc.Block())

        @block.sync
        def _(sp):
            def load_group(n):
                b, g = divmod(n, GROUPS)
                r0 = g * ROWS
                t, s = y[n % 2], y_loaded[n % 2]
                if n >= 2:
                    sp.wait_ge(l0_step, 10 * (n - 1))
                sp.dma_start(t[:, 1:T + 1, 1:D + 1],
                             x[b, r0:r0 + ROWS, :].rearrange("(p t) d -> p t d", t=T)).then_inc(s, 16)
                if g == 0:
                    sp.dma_start(t[0:1, 0, 1:D + 1], x[b, 1:2, :]).then_inc(s, 16)
                    sp.dma_start(t[1:16, 0, 1:D + 1],
                                 x[b, T - 1:T - 1 + 15 * T, :].rearrange("(p t) d -> p t d", t=T)[:, 0, :]
                                 ).then_inc(s, 16)
                    sp.dma_start(t[16:P, 0, 1:D + 1],
                                 x[b, 16 * T - 1:ROWS - 1, :].rearrange("(p t) d -> p t d", t=T)[:, 0, :]
                                 ).then_inc(s, 16)
                else:
                    sp.dma_start(t[:, 0, 1:D + 1],
                                 x[b, r0 - 1:r0 - 1 + ROWS, :].rearrange("(p t) d -> p t d", t=T)[:, 0, :]
                                 ).then_inc(s, 16)
                if g == GROUPS - 1:
                    sp.dma_start(t[P - 1:P, T + 1, 1:D + 1], x[b, S - 2:S - 1, :]).then_inc(s, 16)
                    sp.dma_start(t[P - 16:P - 1, T + 1, 1:D + 1],
                                 x[b, S - 16 * T + T:S, :].rearrange("(p t) d -> p t d", t=T)[:, 0, :]
                                 ).then_inc(s, 16)
                    sp.dma_start(t[0:P - 16, T + 1, 1:D + 1],
                                 x[b, r0 + T:r0 + T + (P - 16) * T, :].rearrange("(p t) d -> p t d", t=T)[:, 0, :]
                                 ).then_inc(s, 16)
                else:
                    sp.dma_start(t[:, T + 1, 1:D + 1],
                                 x[b, r0 + T:r0 + T + ROWS, :].rearrange("(p t) d -> p t d", t=T)[:, 0, :]
                                 ).then_inc(s, 16)

            def load_weights(b):
                cat = sp.value_load(idx[0:1, b:b + 1], min_val=0, max_val=cat_w.shape[0] - 1)
                lang = sp.value_load(idx[0:1, BATCH + b:BATCH + b + 1], min_val=0, max_val=lora_a.shape[0] - 1)
                if b:
                    wait_piece_read(sp, PIECES * (b - 1) + 9)
                    sp.wait_ge(g_split, (KC + 1) * b)
                sp.dma_start(wg, cat_w[bass.ds(cat, 1)].rearrange("a (c p) o -> p (a c) o", p=P)
                             ).then_inc(w_loaded[b], 16)
                sp.dma_start(b_raw[b], lora_b[bass.ds(lang, 1)].rearrange("a (c p) r -> p (a c) r", p=P)
                             ).then_inc(w_loaded[b], 16)
                if b == 0:
                    sp.wait_ge(zeroed, 1)
                for i in range(4):
                    sp.dma_start(a_raw[b][32 * i:32 * i + RANK, :],
                                 lora_a[bass.ds(lang, 1)].rearrange("a r d -> (a r) d")
                                 ).then_inc(w_loaded[b], 16)
                sp.dma_start(b_bc[b], cat_b[bass.ds(cat, 1)].to_broadcast([P, D])).then_inc(w_loaded[b], 16)

            def load_embed(b):
                lang = sp.value_load(idx[0:1, BATCH + b:BATCH + b + 1], min_val=0, max_val=lora_a.shape[0] - 1)
                sp.dma_start(vec_rows[b * KC:(b + 1) * KC, :],
                             lang_embed[bass.ds(lang, 1)].rearrange("a (c p) -> (a c) p", p=P)
                             ).then_inc(vec_loaded, 16)

            sp.dma_start(idx[0:1, 0:BATCH], cat_ids.rearrange("(a n) -> a n", a=1)).then_inc(idx_loaded, 16)
            sp.dma_start(idx[0:1, BATCH:2 * BATCH], lang_ids.rearrange("(a n) -> a n", a=1)).then_inc(idx_loaded, 16)
            load_group(0)
            sp.wait_ge(idx_loaded, 32)
            for b in range(BATCH):
                load_embed(b)
            load_weights(0)
            sp.dma_start(pid_i[:], prompt_ids.rearrange("(a n) -> a n", a=1).to_broadcast([P, BATCH])
                         ).then_inc(small_loaded, 16)
            sp.dma_start(w1_sb[:], w1.rearrange("(c p) a -> p c a", p=P)).then_inc(small_loaded, 16)
            for n in range(1, 4):
                load_group(n)
            load_weights(1)
            for n in range(4, NG):
                load_group(n)

        @block.gpsimd
        def _(pool):
            steps = [0]

            def step(ins):
                steps[0] += 1
                ins.then_inc(pool_step, 1)

            def link(ins):
                step(ins)
                pool.wait_ge(pool_step, steps[0])

            for b in range(BATCH):
                step(pool.memset(l1w[b], 0.0))
                step(pool.memset(a_raw[b], 0.0))
            pool.wait_ge(pool_step, steps[0])
            pool.memset(ident[:], 0.0).then_inc(zeroed, 1)
            step(pool.memset(sel_f, 0.0))
            pool.wait_ge(zeroed, 1)
            link(pool.affine_select(out=ident[:], in_=ident[:], compare_op=ALU.not_equal, fill=1.0,
                                    base=0, pattern=[[-1, P]], channel_multiplier=1))
            for i, at_row in ((0, RANK), (0, 32 + RANK), (1, 0), (1, 32)):
                link(pool.affine_select(out=sel_f[:, i, :], in_=sel_f[:, i, :], compare_op=ALU.not_equal, fill=1.0,
                                        base=-at_row, pattern=[[0, P]], channel_multiplier=1))
            step(pool.memset(ones_r[:].bitcast(F32), 1.0))
            link(pool.memset(ones[:], 1.0))
            pool.engine_nop().then_inc(consts_made, 1)

            def pads(n):
                pool.wait_ge(y_loaded[n % 2], y_count(n))
                pool.tensor_copy(y[n % 2][:, 1:T + 1, 0:D + 2:D + 1],
                                 y[n % 2][:, 1:T + 1, 2:D:D - 3]).then_inc(pads_made, 1)

            pads(0)
            step(pool.memset(below, 0.0))
            step(pool.memset(above, 0.0))
            step(pool.memset(rep[:], 0.0))
            step(pool.memset(ew[:].bitcast(F32), 0.0))
            step(pool.memset(e_quad[:], 0.0))
            pool.wait_ge(pool_step, steps[0])
            step(pool.affine_select(out=below, in_=below, compare_op=ALU.is_ge, fill=1.0,
                                    base=0, pattern=[[-1, P]], channel_multiplier=1))
            step(pool.affine_select(out=above, in_=above, compare_op=ALU.is_ge, fill=1.0,
                                    base=0, pattern=[[1, P]], channel_multiplier=-1))
            pads(1)
            step(pool.affine_select(out=rep[:].rearrange("q (a m) -> q a m", m=NBLK),
                                    in_=rep[:].rearrange("q (a m) -> q a m", m=NBLK),
                                    compare_op=ALU.not_equal, fill=1.0,
                                    base=0, pattern=[[0, P // NBLK], [-1, NBLK]], channel_multiplier=1))
            link(pool.iota(row_no[:], [[P, NBLK]], base=1, channel_multiplier=1))
            link(pool.tensor_copy(row_nof[:], row_no[:]))
            pool.wait_ge(small_loaded, 32)
            link(pool.tensor_copy(pidf[:], pid_i[:]))
            link(pool.tensor_scalar(kind[:, 0, :], pidf[:], 0.0, None, ALU.is_equal))
            link(pool.tensor_scalar(kind[:, 1, :], pidf[:], 1.0, None, ALU.is_equal))
            link(pool.tensor_tensor(kind[:, 2, :], kind[:, 0, :], kind[:, 1, :], ALU.add))
            link(pool.tensor_scalar(kind[:, 2, :], kind[:, 2, :], -1.0, 1.0, ALU.mult, ALU.add))
            link(pool.tensor_scalar(pen[:, 0, :], kind[:, 1, :], NEG, None, ALU.mult))
            link(pool.tensor_scalar(pen[:, 1, :], kind[:, 2, :], NEG, None, ALU.mult))
            link(pool.tensor_scalar(pen[:, 2, :], kind[:, 0, :], NEG, None, ALU.mult))
            link(pool.tensor_tensor(count_ab[:, 0, :], kind[:, 0, :], kind[:, 1, :], ALU.subtract))
            link(pool.tensor_scalar(count_ab[:, 1, :], kind[:, 1, :], float(S + 1), None, ALU.mult))
            link(pool.tensor_scalar(count_ab[:, 2, :], kind[:, 2, :], float(S - 1), None, ALU.mult))
            link(pool.tensor_tensor(count_ab[:, 1, :], count_ab[:, 1, :], count_ab[:, 2, :], ALU.add))
            n = NBLK
            for b in range(BATCH):
                link(pool.tensor_scalar(count[:, b, :], row_nof[:], count_ab[:, 0, b:b + 1], count_ab[:, 1, b:b + 1],
                                        ALU.mult, ALU.add))
                for m, parts, w in ((mask[:, b, :], ((below, 0), (ident, 1), (above, 2)), P),
                                    (bm[:, b, :], ((below, 0), (ident, NEG), (above, 2)), n),
                                    (bmt[:, b, :], ((below, 2), (ident, NEG), (above, 0)), n)):
                    for i, (c, by) in enumerate(parts):
                        by = by if by == NEG else pen[0:w, by, b:b + 1]
                        d = m if i == 0 else pool_tmp[0:w, 0:w]
                        link(pool.tensor_scalar(d, c[0:w, 0:w], by, None, ALU.mult))
                        if i:
                            link(pool.tensor_tensor(m, m, d, ALU.add))
                pads(2 + b)
            pool.engine_nop().then_inc(masks_made, 1)

            def piece_low(b, i):
                pool.wait_ge(piece_hi, 7 * b + i + 1)
                if i == 1:
                    pool.tensor_tensor(c_st[b][32:64, :], cbias[b][32:64, :], c_st[b][32:64, :].bitcast(F32),
                                       ALU.subtract).then_inc(g_split, 1)
                    pool.wait_ge(g_split, (KC + 1) * b + 1)
                else:
                    pool.tensor_tensor(g_lo[b][:, i - 2, :], wg[:, i - 2, :], g_hi[b][:, i - 2, :].bitcast(F32),
                                       ALU.subtract).then_inc(g_split, 1)

            for i in range(1, 6):
                piece_low(1, i)
                if i == 3:
                    pads(2 + BATCH)
            for n in range(3 + BATCH, NG):
                pads(n)

            def weights_of_sums(b):
                pool.wait_ge(e_split, b + 1)
                if b:
                    pool.wait_ge(sums_made, b)
                for i in range(4):
                    pool.tensor_copy(ew[:, 32 * i::P + 1], e_hi[:].bitcast(F32)).then_inc(ew_made, 1)
                    pool.tensor_copy(ew[:, 32 * i + NBLK::P + 1], e_lo[:].bitcast(F32)).then_inc(ew_made, 1)

            def end_block(blk):
                if shared_end(blk):
                    pool.wait_ge(out_act, count_of(shared_end, blk))
                    pool.tensor_tensor(ot[blk % 4], ot[blk % 4], x3[:, blk, :], ALU.add).then_inc(out_pool, 1)

            weights_of_sums(0)
            for q in range(NBLK):
                end_block(q)
                if q and low_by_pool(NBLK + q - 1):
                    low_part(pool, NBLK + q - 1).then_inc(xl_pool, 1)
                if q == 8:
                    weights_of_sums(1)
            if low_by_pool(2 * NBLK - 1):
                low_part(pool, 2 * NBLK - 1).then_inc(xl_pool, 1)
            for q in range(NBLK, 2 * NBLK):
                end_block(q)
        @block.scalar
        def _(act):
            for i, src in enumerate((z_x, z_y, z_r)):
                act.dma_start(zs[:, i, :], src.rearrange("(a n) -> a n", a=1).to_broadcast([P, BATCH])
                              ).then_inc(zs_loaded, 16)
            for i, src in enumerate((b1, v)):
                act.dma_start(vec_rows[BATCH * KC + i:BATCH * KC + i + 1, :], src.rearrange("(a n) -> a n", a=1)
                              ).then_inc(vec_loaded, 16)

            def make_quad(n, h):
                b = n // GROUPS
                if n == 0 and h == 0:
                    act.wait_ge(coef_made, 1)
                act.wait_ge(pads_made, n + 1)
                if n:
                    act.wait_ge(l0_step, 10 * (n - 1) + 5 * (h + 1))
                act.activation(quad[h][:], y[n % 2][:, 1 + NHALF * h:1 + NHALF * (h + 1), 1:D + 1],
                               ACT.Identity, bias=coef[:, 1, b:b + 1], scale=coef[:, 0, b:b + 1]
                               ).then_inc(quad_made, 1)

            def split_hi(n, c):
                act.wait_ge(transposed, KC * n + c + 1)
                if n >= 2:
                    act.wait_ge(main_made, T * (n - 1))
                act.activation(xt_hi[n % 2][:, c, :], tr_ps[c % 2][:], ACT.Copy).then_inc(hi_made, 1)

            def build_cols(b):
                act.wait_ge(w_loaded[b], 16 * N_WLOAD)
                for i in range(4):
                    act.activation(l1w[b][:, :, 32 * i:32 * i + RANK], b_raw[b], ACT.Copy).then_inc(lhs_cols, 1)
                act.wait_ge(vec_made, 1)
                for i in range(2):
                    act.activation(l1w[b][:, :, 32 * i + RANK:32 * i + RANK + 1],
                                   vec[:, KC * b:KC * (b + 1)].rearrange("p (c o) -> p c o", o=1), ACT.Copy
                                   ).then_inc(lhs_cols, 1)
                if b:
                    act.wait_ge(piece_made, PIECES * (b - 1) + 6)
                act.activation(a_st[:], a_raw[b], ACT.Copy).then_inc(lhs_cols, 1)

            def piece(b, i):
                src = piece_bank(b, i)
                k = PIECES * b + i
                if i == 0:
                    act.wait_ge(piece_made, k + 1)
                    if b:
                        act.wait_ge(piece_made, PIECES * (b - 1) + 6)
                    act.activation(b_st[:], src[:], ACT.Copy).then_inc(piece_hi, 1)
                elif i == 1:
                    wait_piece_read(act, k)
                    act.activation(c_st[b][:], cbias[b][0:64, :], ACT.Copy).then_inc(piece_hi, 1)
                elif i < 6:
                    wait_piece_read(act, k)
                    act.activation(g_hi[b][:, i - 2, :], wg[:, i - 2, :], ACT.Copy).then_inc(piece_hi, 1)
                elif i < 10:
                    act.wait_ge(piece_made, k + 1)
                    if b and i == 6:
                        act.wait_ge(piece_made, PIECES * (b - 1) + 12)
                    act.activation(gt[:, i - 6, :], src[:], ACT.Copy).then_inc(piece_act, 1)
                elif i == 10:
                    act.wait_ge(piece_made, k + 1)
                    act.activation(ct[:], src[:, 0:KC], ACT.Copy).then_inc(piece_act, 1)
                elif i == 11:
                    act.wait_ge(piece_made, k + 1)
                    act.activation(gw_hi[b][:].rearrange("p c a -> p (c a)"), src[:], ACT.Copy).then_inc(piece_hi, 1)
                else:
                    act.wait_ge(piece_made, k + 1)
                    act.activation(pbias[:, b:b + 1], src[:, 0:1], ACT.Identity,
                                   bias=vec[:, BATCH * KC:BATCH * KC + 1]).then_inc(piece_act, 1)

            def tanh(n):
                b = n // GROUPS
                act.wait_ge(pre_made, n + 1)
                if n % GROUPS == 0:
                    wait_piece_read(act, PIECES * (b + 1) - 1)
                if n:
                    act.wait_ge(score_made, n)
                act.activation(h_t[:], pre_ps[:], ACT.Tanh, bias=pbias[:, b:b + 1]).then_inc(tanh_made, 1)

            def take_block(blk):
                act.wait_ge(main_made, blk + 1)
                if blk == 15:
                    wait_piece_read(act, 2 * PIECES - 3)
                if blk == 16:
                    wait_piece_read(act, 2 * PIECES - 1)
                    act.wait_ge(masks_made, 1)
                act.activation(x3[:, blk, :], main_ps[blk % 3][:], ACT.Copy).then_inc(x3_made, 1)

            def high_part(blk):
                q = blk % NBLK
                if blk == 0:
                    act.wait_ge(l0_step, 10 * NG)
                if blk >= NBLK:
                    act.wait_ge(pooled, blk - NBLK + 1)
                wait_x3(act, blk)
                act.activation(xh[:, q, :], x3[:, blk, :], ACT.Copy).then_inc(xh_made, 1)

            def soft_exp(b):
                act.wait_ge(soft_dve, 3 * b + 3)
                act.activation(e_f[:], esub[:], ACT.Exp).then_inc(e_made, 1)

            def zb_parts(b):
                act.wait_ge(soft_pe, 3 * b + 3)
                act.activation(zb[:, b, :], misc[:, 0:2], ACT.Copy).then_inc(zb_hi, 1)

            def chunk_exp(b, j):
                act.wait_ge(arg_made, 4 * b + j + 1)
                for i in (1, 0):
                    t = pu[:, j % 2, i, :, :]
                    act.activation(t, t, ACT.Exp).then_inc(exp_made, 1)
                if b and j == 0:
                    act.wait_ge(main_made, T * NG)
                c = slice(4 * j, 4 * j + 4)
                act.wait_ge(exp_made, 8 * b + 2 * j + 1)
                act.activation(us[b][:, c, :], pu[:, j % 2, 1, :, :], ACT.Copy).then_inc(wt_hi, 1)
                act.wait_ge(exp_made, 8 * b + 2 * j + 2)
                act.activation(ph[b][:, c, :], pu[:, j % 2, 0, :, :], ACT.Copy).then_inc(wt_hi, 1)

            def sums_hi(b):
                act.wait_ge(sums_made, b + 1)
                if b:
                    act.wait_ge(pooled, NBLK * b)
                act.activation(cs[:], sum_ps[:], ACT.Copy).then_inc(cs_hi, 1)

            def end_block(blk):
                if not shared_end(blk):
                    return
                b, q = divmod(blk, NBLK)
                act.wait_ge(pooled, blk + 1)
                act.wait_ge(rz_made, blk // 4 + 1)
                if blk >= 4:
                    act.wait_ge(out_stored[blk % 4], 16 * (blk // 4))
                act.activation(ot[blk % 4], main_ps[blk % 3][:], ACT.Copy, scale=rz[:, b, q:q + 1]
                               ).then_inc(out_act, 1)

            make_quad(0, 0)
            make_quad(0, 1)
            build_cols(0)
            make_quad(1, 0)
            piece(0, 0)
            for c in range(KC):
                split_hi(0, c)
            make_quad(1, 1)
            for i in range(1, 6):
                piece(0, i)
            for n in range(NG):
                for k in range(T):
                    if n == 0:
                        for i in LEAD_PIECES[k]:
                            piece(0, i)
                    if n + 1 < NG and k in turn_at(n):
                        for c in turn_at(n)[k]:
                            split_hi(n + 1, c)
                    if k == 0 and 1 <= n < NG - 2:
                        make_quad(n + 2, 1)
                    if k == 0 and n:
                        tanh(n)
                    if 1 <= n < 4:
                        for i in NEXT_PIECES[n - 1][k]:
                            piece(1, i)
                    take_block(T * n + k)
                    if n == 0 and k in (2, 3):
                        make_quad(2, k - 2)
                    if k == T - 1 and n + 3 < NG:
                        make_quad(n + 3, 0)
                    if n == NG - 2:
                        for q in range(4 * k, 4 * k + 4):
                            high_part(q)
                        if k == 2:
                            soft_exp(0)
                        if k == 3:
                            zb_parts(0)
                    if n == NG - 1:
                        chunk_exp(0, k)
                if n == 0:
                    tanh(0)
                    build_cols(1)

            sums_hi(0)
            soft_exp(1)
            for q in range(NBLK):
                end_block(q)
                if q == 2:
                    zb_parts(1)
                if q >= 1:
                    high_part(NBLK + q - 1)
                if q % 3 == 2 and q >= 5:
                    chunk_exp(1, q // 3 - 1)
            high_part(2 * NBLK - 1)
            sums_hi(1)
            for q in range(NBLK, 2 * NBLK):
                end_block(q)

        @block.tensor
        def _(pe):
            def piece(b, i):
                k = PIECES * b + i
                o = piece_bank(b, i)
                if b == 0:
                    if i >= 4:
                        wait_piece_read(pe, i - (4 if i < 6 else 2))
                    if i:
                        wait_piece_read(pe, {1: 0, 2: 0, 3: 0, 4: 0, 5: 0, 6: 5, 7: 5, 8: 5, 9: 5,
                                             10: 1, 11: 9, 12: 10}[i])
                else:
                    wait_piece_read(pe, k - 1)
                if i == 0:
                    pe.wait_ge(lhs_cols, 7 * (b + 1))
                    pe.wait_ge(lhs_built, b + 1)
                    for c in range(KC):
                        m = pe.matmul(o[:], l1w[b][:, c, :], wg[:, c, :], start=(c == 0), stop=(c == KC - 1))
                elif i == 1:
                    m = pe.matmul(o[:], sel[:, 0, :], b_st[:], start=True, stop=True)
                elif i < 6:
                    c = i - 2
                    m = pe.matmul(o[:], a_st[:, c * P:(c + 1) * P], b_st[:], start=True, stop=True)
                elif i < 10:
                    mc = i - 6
                    for c in range(KC):
                        m = pe.transpose(o[:, c * P:(c + 1) * P], wg[:, c, mc * P:(mc + 1) * P], ident[:])
                elif i == 10:
                    for c in range(KC):
                        m = pe.matmul(o[:, c:c + 1], cbias[b][0:1, c * P:(c + 1) * P], ones[0:1, 0:1],
                                      start=True, stop=True)
                elif i == 11:
                    for c in range(KC):
                        for mc in range(KC):
                            m = pe.matmul(o[:, c * P:(c + 1) * P], gt[:, mc, c * P:(c + 1) * P],
                                          w1_sb[:, mc, :], start=(mc == 0), stop=(mc == KC - 1))
                else:
                    for mc in range(KC):
                        m = pe.matmul(o[:, 0:1], w1_sb[:, mc, :], ct[:, mc:mc + 1],
                                      start=(mc == 0), stop=(mc == KC - 1))
                m.then_inc(piece_made, 1)

            def turn_chunk(n, c):
                if c == 0:
                    pe.wait_ge(l0_step, 10 * (n + 1))
                k = KC * n + c
                if k >= 2:
                    pe.wait_ge(lo_made, k - 1)
                rows = tr_ps[c % 2][:].rearrange("d (p t) -> d t p", t=T)
                for t in range(T):
                    m = pe.transpose(rows[:, t, :], x1[t // NHALF][:, t % NHALF, c * P:(c + 1) * P], ident[:])
                m.then_inc(transposed, 1)

            def three(out, hi, lo, r_hi, r_lo, first, last):
                pe.matmul(out, hi, r_hi, start=first, stop=False)
                pe.matmul(out, hi, r_lo, start=False, stop=False)
                return pe.matmul(out, lo, r_hi, start=False, stop=last)

            def pre_group(n):
                b, i = n // GROUPS, n % 2
                if n % GROUPS == 0:
                    wait_piece_read(pe, PIECES * b + 11)
                    wait_piece_read(pe, PIECES * b + 12)
                pe.wait_ge(lo_made, KC * (n + 1))
                if n:
                    pe.wait_ge(tanh_made, n)
                for c in range(KC):
                    m = three(pre_ps[:], gw_hi[b][:, c, :], gw_lo[b][:, c, :], xt_hi[i][:, c, :], xt_lo[i][:, c, :],
                              c == 0, c == KC - 1)
                m.then_inc(pre_made, 1)

            def main_block(n, k):
                b, i, blk = n // GROUPS, n % 2, T * n + k
                if k == 0:
                    pe.wait_ge(lo_made, KC * (n + 1))
                    if n % GROUPS == 0:
                        pe.wait_ge(g_split, (KC + 1) * (b + 1) if n else 1)
                if blk >= 3:
                    wait_x3(pe, blk - 3)
                rows = slice(k * P, (k + 1) * P)
                pe.matmul(main_ps[blk % 3][:], sel[0:64, 1, :], c_st[b][:], start=True, stop=False)
                for c in range(KC):
                    if blk == 0:
                        pe.wait_ge(g_split, 2 + c)
                    m = three(main_ps[blk % 3][:], xt_hi[i][:, c, rows], xt_lo[i][:, c, rows],
                              g_hi[b][:, c, :], g_lo[b][:, c, :], False, c == KC - 1)
                m.then_inc(main_made, 1)

            def score_group(n):
                pe.wait_ge(tanh_made, n + 1)
                if n == GROUPS:
                    pe.wait_ge(soft_dve, 1)
                for k in range(T):
                    m = pe.matmul(sc_ps[:, T * n + k:T * n + k + 1], h_t[:, k * P:(k + 1) * P],
                                  vec[:, BATCH * KC + 1:BATCH * KC + 2], start=True, stop=True)
                m.then_inc(score_made, 1)

            def soft_turn(b):
                pe.wait_ge(soft_dve, 3 * b + 1)
                if b:
                    pe.wait_ge(arg_made, 4 * b)
                pe.transpose(misc[0:NBLK, 0:P], sc[:, b, :], ident[:]).then_inc(soft_pe, 1)

            def soft_spread(b):
                pe.wait_ge(soft_dve, 3 * b + 2)
                pe.matmul(misc[:, 0:NBLK], ones[0:NBLK, :], diagb[:], start=True, stop=True)
                pe.matmul(misc[:, NBLK:2 * NBLK], rep[:], xb16[:], start=True, stop=True).then_inc(soft_pe, 1)

            def soft_zb(b):
                pe.wait_ge(e_spread, b + 1)
                pe.wait_ge(soft_dve, 3 * b + 3)
                pe.matmul(misc[:, 0:2], e_quad[:], ones[:, 0:2], start=True, stop=True).then_inc(soft_pe, 1)

            def chunk_max(b, j):
                if j == 0:
                    pe.wait_ge(soft_dve, 3 * b + 3)
                    pe.wait_ge(zb_made, b + 1)
                if 4 * b + j >= 2:
                    pe.wait_ge(arg_made, 4 * b + j - 1)
                for k in range(4):
                    q = 4 * j + k
                    m = pe.matmul(nm_ps[j % 2][:, k * P:(k + 1) * P],
                                  pick[:, q:q + 1].to_broadcast([32 + NBLK, P]), nm_st[:], start=True, stop=True)
                m.then_inc(nm_made, 1)

            def chunk_sum(b, j):
                k = 4 * b + j
                pe.wait_ge(wt_lo, 2 * (k + 1))
                if j == 0:
                    pe.wait_ge(zb_made, b + 1)
                if k:
                    pe.wait_ge(rz_made, k)
                for q in range(4 * j, 4 * j + 4):
                    o = z_ps[:, 2 * q:2 * q + 2]
                    pe.matmul(o, ph[b][:, q, :], ones_r[:], start=True, stop=False)
                    pe.matmul(o, pl[b][:, q, :], ones_r[:], start=False, stop=False)
                    m = pe.matmul(o, us[b][:, q, :], zb[:, b, :], start=False, stop=True)
                m.then_inc(z_made, 1)

            def sums(b, q):
                if q == 0:
                    pe.wait_ge(ew_made, 8 * (b + 1))
                    if b == 0:
                        pe.wait_ge(tanh_made, NG)
                    else:
                        pe.wait_ge(cs_made, b)
                wait_low(pe, NBLK * b + q)
                lhs = ew[:, q * P:(q + 1) * P]
                pe.matmul(sum_ps[:], lhs, xh[:, q, :], start=(q == 0), stop=False)
                m = pe.matmul(sum_ps[:], lhs, xl[q], start=False, stop=(q == NBLK - 1))
                if q == NBLK - 1:
                    m.then_inc(sums_made, 1)

            def pool_own(b, q):
                blk = NBLK * b + q
                if blk < 3:
                    wait_x3(pe, BATCH * NBLK - 3 + (blk + 1) % 3)
                else:
                    wait_bank_taken(pe, blk - 3)
                o = main_ps[blk % 3][:]
                pe.matmul(o, ph[b][:, q, :], xh[:, q, :], start=True, stop=False)
                pe.matmul(o, ph[b][:, q, :], xl[q], start=False, stop=False)
                pe.matmul(o, pl[b][:, q, :], xh[:, q, :], start=False, stop=False)

            def pool_others(b, q):
                if q == 0:
                    pe.wait_ge(cs_made, b + 1)
                pe.matmul(main_ps[(NBLK * b + q) % 3][:], us[b][:, q, :], cs[:], start=False, stop=True
                          ).then_inc(pooled, 1)

            def pool_blocks(b, between):
                chunk_sum(b, 0)
                for q in range(3):
                    pool_own(b, q)
                for q in range(3):
                    pool_others(b, q)
                between(2)
                for q in range(3, NBLK):
                    if q % 4 == 0:
                        chunk_sum(b, q // 4)
                    pool_own(b, q)
                    pool_others(b, q)
                    between(q)

            pe.wait_ge(consts_made, 1)
            pe.wait_ge(vec_loaded, 16 * N_VEC)
            pe.transpose(tr_ps[0][:, 0:BATCH * KC + 2], vec_rows, ident[0:BATCH * KC + 2, 0:BATCH * KC + 2]
                         ).then_inc(vec_rows_turned, 1)
            pe.wait_ge(vec_made, 1)
            piece(0, 0)
            for c in range(KC):
                turn_chunk(0, c)
            for i in range(1, 6):
                piece(0, i)
            pe.wait_ge(small_loaded, 32)
            for n in range(NG):
                if n:
                    pre_group(n)
                for k in range(T):
                    main_block(n, k)
                    if n == 0:
                        for i in LEAD_PIECES[k]:
                            piece(0, i)
                    if n + 1 < NG and k in turn_at(n):
                        for c in turn_at(n)[k]:
                            turn_chunk(n + 1, c)
                    if 1 <= n < 4:
                        for i in NEXT_PIECES[n - 1][k]:
                            piece(1, i)
                    if n == 1 and k == 0:
                        score_group(0)
                    if n and k == 1:
                        score_group(n)
                    if n == NG - 2:
                        if k == 0:
                            soft_turn(0)
                        elif k == 1:
                            soft_spread(0)
                        elif k == 3:
                            soft_zb(0)
                    if n == NG - 1:
                        chunk_max(0, k)
                if n == 0:
                    pre_group(0)

            for q in range(NBLK):
                sums(0, q)
                if q == 4:
                    soft_turn(1)
                if q == 10:
                    soft_spread(1)

            def between(q):
                if q == 2:
                    soft_zb(1)
                if q % 3 == 1 and q // 3 - 1 < 4:
                    chunk_max(1, q // 3 - 1)

            pool_blocks(0, between)
            for q in range(NBLK):
                sums(1, q)
            pool_blocks(1, lambda q: None)

        @block.vector
        def _(dve):
            chain = [0]

            def link(ins):
                chain[0] += 1
                ins.then_inc(dve_step, 1)
                dve.wait_ge(dve_step, chain[0])

            def build_lhs(b):
                dve.wait_ge(w_loaded[b], 16 * N_WLOAD)
                for c in range(KC):
                    d = wg[:, c, c * P:(c + 1) * P]
                    dve.tensor_tensor(d, d, ident[:], ALU.add).then_inc(dve_step, 1)
                chain[0] += KC
                dve.wait_ge(lhs_cols, 7 * (b + 1))
                dve.tensor_tensor(a_st[64:P, :], a_raw[b][64:P, :], a_st[64:P, :].bitcast(F32), ALU.subtract
                                  ).then_inc(lhs_built, 1)

            def piece(b, i):
                k = PIECES * b + i
                src = piece_bank(b, i)
                if read_by_act(k):
                    return
                dve.wait_ge(piece_made, k + 1)
                if i == 0:
                    dve.wait_ge(piece_hi, 7 * b + 1)
                    for s in (32, 96):
                        m = dve.tensor_tensor(b_st[s:s + 32, :], src[s:s + 32, :], b_st[s:s + 32, :].bitcast(F32),
                                              ALU.subtract)
                elif i == 1:
                    m = dve.tensor_tensor(cbias[b], src[:], b_bc[b], ALU.add)
                elif i < 6:
                    m = dve.tensor_tensor(wg[:, i - 2, :], src[:], wg[:, i - 2, :], ALU.add)
                elif i == 11:
                    dve.wait_ge(piece_hi, 7 * b + 7)
                    m = dve.tensor_tensor(gw_lo[b][:].rearrange("p c a -> p (c a)"), src[:],
                                          gw_hi[b][:].rearrange("p c a -> p (c a)").bitcast(F32), ALU.subtract)
                m.then_inc(piece_dve, 1)

            def piece_low(i):
                dve.wait_ge(piece_hi, i + 1)
                if i == 1:
                    dve.tensor_tensor(c_st[0][32:64, :], cbias[0][32:64, :], c_st[0][32:64, :].bitcast(F32),
                                      ALU.subtract).then_inc(g_split, 1)
                else:
                    dve.tensor_tensor(g_lo[0][:, i - 2, :], wg[:, i - 2, :], g_hi[0][:, i - 2, :].bitcast(F32),
                                      ALU.subtract).then_inc(g_split, 1)

            def stencil(n, h, o):
                b = n // GROUPS
                t = y[n % 2]
                r = 1 + NHALF * h
                k = 10 * n + 5 * h
                if k + o:
                    dve.wait_ge(l0_step, k + o)
                if o == 0:
                    dve.wait_ge(pads_made, n + 1)
                    m = dve.tensor_tensor(lap[:], t[:, r:r + NHALF, 0:D], t[:, r:r + NHALF, 2:D + 2], ALU.add)
                elif o == 1:
                    dve.wait_ge(quad_made, 2 * n + h + 1)
                    m = dve.tensor_tensor(quad[h][:], quad[h][:], t[:, r:r + NHALF, 1:D + 1], ALU.mult)
                elif o == 2:
                    m = dve.scalar_tensor_tensor(lap[:], lap[:], zs[:, 0, b:b + 1], quad[h][:], ALU.mult, ALU.add)
                elif o == 3:
                    m = dve.tensor_tensor(quad[h][:], t[:, r - 1:r - 1 + NHALF, 1:D + 1],
                                          t[:, r + 1:r + 1 + NHALF, 1:D + 1], ALU.add)
                else:
                    if n:
                        dve.wait_ge(transposed, KC * n)
                    m = dve.scalar_tensor_tensor(x1[h][:], quad[h][:], zs[:, 1, b:b + 1], lap[:], ALU.mult, ALU.add)
                m.then_inc(l0_step, 1)

            def split_lo(n, c):
                dve.wait_ge(hi_made, KC * n + c + 1)
                if n >= 2:
                    dve.wait_ge(main_made, T * (n - 1))
                dve.tensor_tensor(xt_lo[n % 2][:, c, :], tr_ps[c % 2][:], xt_hi[n % 2][:, c, :].bitcast(F32),
                                  ALU.subtract).then_inc(lo_made, 1)

            def soft_take(b):
                dve.wait_ge(score_made, GROUPS * (b + 1))
                dve.tensor_copy(sc[:, b, :], sc_ps[:, b * NBLK:(b + 1) * NBLK]).then_inc(soft_dve, 1)

            def soft_scan(b):
                dve.wait_ge(soft_pe, 3 * b + 1)
                if b == 0:
                    dve.wait_ge(masks_made, 1)
                    link(dve.memset(pmx[:, 0:1], NEG))
                    link(dve.memset(sfx[:, P:P + 1], NEG))
                    link(dve.memset(nm_st[:].bitcast(F32), 0.0))
                link(dve.tensor_copy(s16[:], misc[0:NBLK, 0:P]))
                dve.tensor_tensor_scan(sfx[:, P - 1::-1], s16[:, P - 1::-1], s16[:, P - 1::-1], NEG,
                                       ALU.max, ALU.max).then_inc(dve_step, 1)
                chain[0] += 1
                link(dve.tensor_tensor_scan(pmx[:, 1:P + 1], s16[:], s16[:], NEG, ALU.max, ALU.max))
                dve.tensor_scalar(diagb[:], ident[0:NBLK, 0:NBLK], pmx[:, P:P + 1], None, ALU.mult
                                  ).then_inc(dve_step, 1)
                chain[0] += 1
                dve.wait_ge(dve_step, chain[0])
                dve.tensor_scalar(xb16[:], bm[:, b, :], pmx[:, P:P + 1], None, ALU.add).then_inc(soft_dve, 1)

            def soft_max(b):
                dve.wait_ge(soft_pe, 3 * b + 2)
                link(dve.tensor_tensor(esub[:], sc[:, b, :], misc[:, 0:NBLK], ALU.subtract))
                link(dve.tensor_copy(bmb[:], misc[:, NBLK:2 * NBLK]))
                link(dve.tensor_tensor(tmp16[:], misc[0:NBLK, 0:NBLK], bmt[:, b, :], ALU.add))
                link(dve.reduce_max(be[:], tmp16[:], AX_X))
                link(dve.tensor_scalar(mrow[:], pmx[:, 0:P], pen[0:NBLK, 0, b:b + 1], be[:], ALU.add, ALU.max))
                link(dve.scalar_tensor_tensor(mrow[:], sfx[:, 1:P + 1], pen[0:NBLK, 2, b:b + 1], mrow[:],
                                              ALU.add, ALU.max))
                link(dve.scalar_tensor_tensor(mrow[:], s16[:], pen[0:NBLK, 1, b:b + 1], mrow[:], ALU.add, ALU.max))
                if b:
                    dve.wait_ge(nm_made, 4 * b)
                link(dve.tensor_scalar(nm_st[0:NBLK, :], mrow[:], -1.0, None, ALU.mult))
                dve.scalar_tensor_tensor(nm_st[32:32 + NBLK, :], mrow[:], -1.0, nm_st[0:NBLK, :].bitcast(F32),
                                         ALU.mult, ALU.subtract).then_inc(soft_dve, 1)

            def soft_split(b):
                dve.wait_ge(e_made, b + 1)
                if b:
                    dve.wait_ge(soft_pe, 3 * b)
                dve.tensor_copy(e_quad[:].rearrange("p (g m) -> p g m", g=4)[:, :, 0:NBLK],
                                e_f[:].rearrange("p (o m) -> p o m", o=1).to_broadcast([P, 4, NBLK])
                                ).then_inc(e_spread, 1)
                if b:
                    dve.wait_ge(ew_made, 8 * b)
                link(dve.tensor_copy(e_hi[:], e_f[:]))
                dve.tensor_tensor(e_lo[:], e_f[:], e_hi[:].bitcast(F32), ALU.subtract).then_inc(e_split, 1)

            def zb_lows(b):
                dve.wait_ge(zb_hi, b + 1)
                for i in (32, 96):
                    m = dve.tensor_tensor(zb[i:i + 32, b, :], misc[i:i + 32, 0:2], zb[i:i + 32, b, :].bitcast(F32),
                                          ALU.subtract)
                m.then_inc(zb_made, 1)

            def chunk_args(b, j):
                dve.wait_ge(nm_made, 4 * b + j + 1)
                k = 4 * b + j
                if k >= 2:
                    dve.wait_ge(wt_lo, 2 * (k - 1))
                p = pu[:, j % 2, 0, :, :]
                for i in range(4):
                    dve.scalar_tensor_tensor(p[:, i, :], nm_ps[j % 2][:, i * P:(i + 1) * P],
                                             sc[:, b, 4 * j + i:4 * j + i + 1], mask[:, b, :], ALU.add, ALU.add)
                dve.tensor_tensor(pu[:, j % 2, 1, :, :], nm_ps[j % 2][:].rearrange("p (q i) -> p q i", q=4),
                                  bmb[:, 4 * j:4 * j + 4].rearrange("p (q o) -> p q o", o=1).to_broadcast([P, 4, P]),
                                  ALU.add).then_inc(arg_made, 1)

            def chunk_rz(b, j):
                dve.wait_ge(z_made, 4 * b + j + 1)
                c = slice(4 * j, 4 * j + 4)
                link(dve.tensor_tensor(zc[:, c], z_ps[:, 8 * j:8 * j + 8:2], count[:, b, c], ALU.mult))
                dve.reciprocal(rz[:, b, c], zc[:, c]).then_inc(rz_made, 1)

            def chunk_lo(b, j):
                c = slice(4 * j, 4 * j + 4)
                dve.wait_ge(wt_hi, 2 * (4 * b + j) + 2)
                dve.tensor_tensor(us[b][64:P, c, :], pu[64:P, j % 2, 1, :, :], us[b][64:P, c, :].bitcast(F32),
                                  ALU.subtract).then_inc(wt_lo, 1)
                dve.tensor_tensor(pl[b][:, c, :], pu[:, j % 2, 0, :, :], ph[b][:, c, :].bitcast(F32), ALU.subtract
                                  ).then_inc(wt_lo, 1)

            def sums_lo(b):
                dve.wait_ge(cs_hi, b + 1)
                for s in (32, 96):
                    m = dve.tensor_tensor(cs[s:s + 32, :], sum_ps[s:s + 32, :], cs[s:s + 32, :].bitcast(F32),
                                          ALU.subtract)
                m.then_inc(cs_made, 1)

            def end_block(blk):
                b, q = divmod(blk, NBLK)
                if q % 4 == 0:
                    chunk_rz(b, q // 4)
                if shared_end(blk):
                    return
                dve.wait_ge(pooled, blk + 1)
                dve.wait_ge(rz_made, blk // 4 + 1)
                if blk >= 4:
                    dve.wait_ge(out_stored[blk % 4], 16 * (blk // 4))
                dve.scalar_tensor_tensor(ot[blk % 4], main_ps[blk % 3][:], rz[:, b, q:q + 1], x3[:, blk, :],
                                         ALU.mult, ALU.add).then_inc(out_dve, 1)

            def low(blk):
                if not low_by_pool(blk):
                    low_part(dve, blk).then_inc(xl_dve, 1)

            dve.wait_ge(zs_loaded, 48)
            link(dve.tensor_scalar(coef[:, 0, :], zs[:, 2, :], -1.0, None, ALU.mult))
            link(dve.tensor_tensor(z_sum[:], zs[:, 0, :], zs[:, 1, :], ALU.add))
            link(dve.tensor_scalar(z_sum[:], z_sum[:], -2.0, 1.0, ALU.mult, ALU.add))
            dve.tensor_tensor(coef[:, 1, :], z_sum[:], zs[:, 2, :], ALU.add).then_inc(coef_made, 1)
            dve.wait_ge(consts_made, 1)
            link(dve.tensor_copy(sel[:], sel_f))
            link(dve.memset(pick[:].bitcast(F32), 0.0))
            link(dve.tensor_copy(pick[0:NBLK, :], ident[0:NBLK, 0:NBLK]))
            link(dve.tensor_copy(pick[32:32 + NBLK, :], ident[32:32 + NBLK, 32:32 + NBLK]))
            for o in range(4):
                stencil(0, 0, o)
            dve.wait_ge(vec_rows_turned, 1)
            dve.tensor_copy(vec[:], tr_ps[0][:, 0:BATCH * KC + 2]).then_inc(vec_made, 1)
            stencil(0, 0, 4)
            for o in range(3):
                stencil(0, 1, o)
            build_lhs(0)
            for o in range(3, 5):
                stencil(0, 1, o)
            piece(0, 0)
            for c in range(KC):
                split_lo(0, c)
            piece(0, 1)
            for i in range(2, 6):
                piece(0, i)
                piece_low(i - 1)
            piece_low(5)
            for h in range(2):
                for o in range(5):
                    stencil(1, h, o)
            for n in range(NG):
                ops = [(h, o) for h in range(2) for o in range(5)] if n + 2 < NG else []
                for k in range(T):
                    if n == 0:
                        for i in LEAD_PIECES[k]:
                            piece(0, i)
                    if 1 <= n < 4:
                        for i in NEXT_PIECES[n - 1][k]:
                            if i == 0:
                                piece(1, i)
                    for _ in range((0, 0, 0, 2)[k] if n == 0 else (3, 1, 3, 3)[k]):
                        if ops:
                            stencil(n + 2, *ops.pop(0))
                    if n + 1 < NG and k in turn_at(n):
                        for c in turn_at(n)[k]:
                            split_lo(n + 1, c)
                    if 1 <= n < 4:
                        for i in NEXT_PIECES[n - 1][k]:
                            if i:
                                piece(1, i)
                    if n == GROUPS and k == 0:
                        soft_take(0)
                    if n == NG - 2:
                        if k == 0:
                            soft_scan(0)
                        elif k == 1:
                            soft_max(0)
                        elif k == 3:
                            soft_split(0)
                            for q in range(4):
                                low(q)
                            zb_lows(0)
                    if n == NG - 1:
                        if k:
                            chunk_lo(0, k - 1)
                        chunk_args(0, k)
                        for q in range(4 + 3 * k, 7 + 3 * k):
                            low(q)
                        if k == 2:
                            soft_take(1)
                if n == 0:
                    while ops:
                        stencil(2, *ops.pop(0))
                    build_lhs(1)
            chunk_lo(0, 3)

            soft_scan(1)
            soft_max(1)
            sums_lo(0)
            soft_split(1)
            for q in range(NBLK):
                end_block(q)
                if q == 2:
                    zb_lows(1)
                if q:
                    low(NBLK + q - 1)
                if q % 3 == 1 and 1 <= q // 3 <= 4:
                    chunk_args(1, q // 3 - 1)
                if q % 3 == 0 and 2 <= q // 3 <= 5:
                    chunk_lo(1, q // 3 - 2)
            low(2 * NBLK - 1)
            sums_lo(1)
            for q in range(NBLK, 2 * NBLK):
                end_block(q)

        @block.sync
        def _(sp):
            for blk in range(BATCH * NBLK):
                b, q = divmod(blk, NBLK)
                wait_out(sp, blk)
                sp.dma_start(out[b, q * P:(q + 1) * P, :], ot[blk % 4]).then_inc(out_stored[blk % 4], 16)
            for i in range(4):
                sp.wait_ge(out_stored[i], 16 * (BATCH * NBLK // 4))


POOL_LOWS = tuple(range(17, 32, 2))
SHARED_ENDS = (2, 6, 10, 14)
LEAD_PIECES = [(6, 7), (8, 9), (10, 11), (12,)]
NEXT_PIECES = [[(0,), (1,), (2,), (3,)], [(4,), (5,), (6,), (7,)], [(8,), (9,), (10, 11), (12,)]]

_INS = ["x", "condB_zX", "condB_zY", "condB_zR", "itok_B_0_3", "itok_B_0_30", "itok_B_0_2", "L1_cond_lora_A",
        "L1_cond_lora_B", "L1_cond_lang_embed", "L2_cond_W", "L2_cond_b", "L3_cond_W1", "L3_cond_b1", "L3_cond_v"]


def kernel(**inputs):
    import concourse.bacc as bacc
    from concourse.bass_utils import run_bass_kernel_spmd

    nc = bacc.Bacc("TRN2", target_bir_lowering=False, num_devices=1, dynamic_dma_scratch_size=1024)
    arrays, args = {}, []
    for name in _INS:
        a = np.ascontiguousarray(inputs[name])
        arrays[f"in_{name}"] = a
        args.append(nc.dram_tensor(f"in_{name}", a.shape, mybir.dt.from_np(a.dtype), kind="ExternalInput").ap())
    shape = tuple(inputs["x"].shape)
    args.append(nc.dram_tensor("out", shape, F32, kind="ExternalOutput").ap())
    fused_layers(nc, *args)
    r = run_bass_kernel_spmd(nc, [arrays], core_ids=[0])
    return r.results[0]["out"]
```

```python
from contextlib import ExitStack

import numpy as np

import concourse.bass as bass
from concourse import mybir

F32 = mybir.dt.float32
F32R = mybir.dt.float32r
I32 = mybir.dt.int32
ALU = mybir.AluOpType
ACT = mybir.ActivationFunctionType
AX_X = mybir.AxisListType.X


P = 128
NEG = -1.0e30


def fused_layers(nc, x, z_x, z_y, z_r, lang_ids, cat_ids, prompt_ids, lora_a, lora_b, lang_embed,
                 cat_w, cat_b, w1, b1, v, out):
    BATCH, S, D = x.shape
    RANK = lora_a.shape[1]
    ATT = w1.shape[1]
    KC = D // P
    T = 4
    ROWS = P * T
    GROUPS = S // ROWS
    NG = BATCH * GROUPS
    NBLK = S // P
    NHALF = T // 2
    assert (KC, NBLK, RANK, ATT) == (4, 16, 16, P) and T == KC

    with ExitStack() as ctx:
        def sb(name, shape, dt=F32):
            return ctx.enter_context(nc.sbuf_tensor(name, shape, dt))

        def sem(name):
            return ctx.enter_context(nc.semaphore(name))

        x3 = sb("x3", [P, BATCH * NBLK, D])
        ident = sb("ident", [P, P])
        pick = sb("pick", [32 + NBLK, NBLK], F32R)
        ones = sb("ones", [P, P])
        rep = sb("rep", [NBLK, P])
        sel = sb("sel", [P, 2, P], F32R)
        row_no = sb("row_no", [P, NBLK], I32)
        row_nof = sb("row_nof", [P, NBLK])
        zs = sb("zs", [P, 3, BATCH])
        coef = sb("coef", [P, 2, BATCH])
        pid_i = sb("pid_i", [P, BATCH], I32)
        pidf = sb("pidf", [P, BATCH])
        kind = sb("kind", [P, 3, BATCH])
        pen = sb("pen", [P, 3, BATCH])
        z_sum = sb("z_sum", [P, BATCH])
        count_ab = sb("count_ab", [P, 3, BATCH])
        count = sb("count", [P, BATCH, NBLK])
        mask = sb("mask", [P, BATCH, P])
        bm = sb("bm", [NBLK, BATCH, NBLK])
        bmt = sb("bmt", [NBLK, BATCH, NBLK])
        idx = sb("idx", [1, 2 * BATCH], I32)
        vec = sb("vec", [P, BATCH * KC + 2])
        sc = sb("sc", [P, BATCH, NBLK])
        diagb = sb("diagb", [NBLK, NBLK])
        xb16 = sb("xb16", [NBLK, NBLK])
        tmp16 = sb("tmp16", [NBLK, NBLK])
        be = sb("be", [NBLK, 1])
        e_quad = sb("e_quad", [P, P])
        zb = sb("zb", [P, BATCH, 2], F32R)
        ones_r = sb("ones_r", [P, 2], F32R)
        esub = sb("esub", [P, NBLK])
        e_f = sb("e_f", [P, NBLK])
        nm_st = sb("nm_st", [32 + NBLK, P], F32R)
        e_hi = sb("e_hi", [P, NBLK], F32R)
        e_lo = sb("e_lo", [P, NBLK], F32R)
        bmb = sb("bmb", [P, NBLK])
        zc = sb("zc", [P, NBLK])
        rz = sb("rz", [P, BATCH, NBLK])
        ew = sb("ew", [P, NBLK * P], F32R)
        ph0 = sb("ph0", [P, NBLK, P], F32R)
        pl0 = sb("pl0", [P, NBLK, P], F32R)

        at = [(nc.sbuf_base + 63) // 64 * 64]

        def sb_at(name, shape, dt=F32):
            where = at[0]
            t = nc.alloc_sbuf_tensor_at(name, shape, dt, offset=where)
            at[0] += (int(np.prod(shape[1:])) * 4 + 63) // 64 * 64
            return t, where

        def over(name, shape, dt, where, end):
            assert where + int(np.prod(shape[1:])) * 4 <= end
            return nc.alloc_sbuf_tensor_at(name, shape, dt, offset=where)

        (y0, y_at), (y1, _) = [sb_at(f"y{i}", [P, T + 2, D + 2]) for i in range(2)]
        y = [y0, y1]
        quad = [sb_at(f"quad{i}", [P, NHALF, D])[0] for i in range(2)]
        lap, _ = sb_at("lap", [P, NHALF, D])
        (x1a, x1_at), (x1b, _) = [sb_at(f"x1_{i}", [P, NHALF, D]) for i in range(2)]
        x1 = [x1a, x1b]
        (xh0, xt0_at), (xl0, _) = sb_at("xt_hi0", [P, KC, ROWS], F32R), sb_at("xt_lo0", [P, KC, ROWS], F32R)
        (xh1, xt1_at), (xl1, _) = sb_at("xt_hi1", [P, KC, ROWS], F32R), sb_at("xt_lo1", [P, KC, ROWS], F32R)
        xt_hi, xt_lo = [xh0, xh1], [xl0, xl1]
        xt_end = at[0]
        g_hi, g_lo, gw_hi, gw_lo, g_at = [], [], [], [], []
        for b in range(BATCH):
            g_at.append(at[0])
            g_hi.append(sb_at(f"g_hi{b}", [P, KC, D], F32R)[0])
            g_lo.append(sb_at(f"g_lo{b}", [P, KC, D], F32R)[0])
            gw_hi.append(sb_at(f"gw_hi{b}", [P, KC, ATT], F32R)[0])
            gw_lo.append(sb_at(f"gw_lo{b}", [P, KC, ATT], F32R)[0])
        a_st, _ = sb_at("a_st", [P, D], F32R)
        b_st, _ = sb_at("b_st", [P, D], F32R)
        g_end = at[0]
        w1_sb, _ = sb_at("w1_sb", [P, KC, ATT])
        c_st = [sb_at(f"c_st{b}", [64, D], F32R)[0] for b in range(BATCH)]
        ct, _ = sb_at("ct", [P, KC])
        pbias, _ = sb_at("pbias", [P, BATCH])
        h_t, _ = sb_at("h_t", [P, ROWS])
        assert at[0] <= nc.sbuf_usable_end, at[0] - nc.sbuf_usable_end
        wg = x3[:, 24:24 + KC, :]
        gt = x3[:, 28:28 + KC, :]
        l1w = [x3[:, 22 + b, :].rearrange("p (c m) -> p c m", c=KC) for b in range(BATCH)]
        a_raw = [x3[:, 20 + b, :] for b in range(BATCH)]
        b_bc = [x3[:, 18 + b, :] for b in range(BATCH)]
        b_raw = [x3[:, 17, b * KC * RANK:(b + 1) * KC * RANK].rearrange("p (c r) -> p c r", c=KC)
                 for b in range(BATCH)]
        vec_rows = x3[0:BATCH * KC + 2, 17, 128:256]
        pool_tmp = x3[:, 17, 256:384]
        below, above = x3[:, 16, 0:P], x3[:, 16, P:2 * P]
        sel_f = x3[:, 16, 2 * P:4 * P].rearrange("p (i m) -> p i m", i=2)
        cbias = [x3[:, 14 + b, :] for b in range(BATCH)]

        row = D * 4
        xh = over("xh", [P, NBLK, D], F32R, y_at, x1_at)
        xl_x1 = over("xl_x1", [P, 4, D], F32R, x1_at, xt0_at)
        xl_t0 = over("xl_t0", [P, 8, D], F32R, xt0_at, xt1_at)
        xl_t1 = over("xl_t1", [P, 4, D], F32R, xt1_at, xt_end)
        xl = [(xl_x1, q) if q < 4 else (xl_t0, q - 4) if q < 12 else (xl_t1, q - 12) for q in range(NBLK)]
        xl = [t[:, i, :] for t, i in xl]
        ot_all = over("ot", [P, 4, D], F32, xt1_at + 4 * row, xt_end)
        ot = [ot_all[:, i, :] for i in range(4)]
        spare = g_at[0] + 9 * row
        small = []
        for name, w in (("s16", P), ("pmx", P + 1), ("sfx", P + 1)):
            small.append(over(name, [NBLK, w], F32, spare, g_at[1]))
            spare += (w * 4 + 31) // 32 * 32
        s16, pmx, sfx = small
        cs = over("cs", [P, D], F32R, g_at[0] + 8 * row, g_at[1])
        us0 = over("us0", [P, NBLK, P], F32R, g_at[0], g_at[1])
        pu = over("pu", [P, 2, 2, 4, P], F32, g_at[0] + 4 * row, g_at[0] + 8 * row)
        ph1 = over("ph1", [P, NBLK, P], F32R, g_at[1], g_end)
        pl1 = over("pl1", [P, NBLK, P], F32R, g_at[1] + 4 * row, g_end)
        us1 = over("us1", [P, NBLK, P], F32R, g_at[1] + 8 * row, g_end)
        ph, pl, us = [ph0, ph1], [pl0, pl1], [us0, us1]

        banks = [ctx.enter_context(nc.psum_tensor(f"bank{i}", [P, 512], F32)) for i in range(8)]
        main_ps, pre_ps, tr_ps, sc_ps, misc = banks[0:3], banks[3], banks[4:6], banks[6], banks[7]
        z_ps = tr_ps[0]
        out_ps = main_ps + [sc_ps]
        sum_ps = pre_ps

        def piece_bank(b, i):
            if b:
                return pre_ps if i in IN_PRE_BANK else misc
            return [misc, main_ps[1], main_ps[2], sc_ps][i % 4] if i < 6 else [misc, sc_ps][i % 2]

        idx_loaded = sem("idx_loaded")
        zs_loaded = sem("zs_loaded")
        vec_loaded = sem("vec_loaded")
        small_loaded = sem("small_loaded")
        w_loaded = [sem(f"w_loaded{b}") for b in range(BATCH)]
        y_loaded = [sem(f"y_loaded{i}") for i in range(2)]
        out_stored = [sem(f"out_stored{i}") for i in range(4)]
        pool_step = sem("pool_step")
        zeroed = sem("zeroed")
        consts_made = sem("consts_made")
        masks_made = sem("masks_made")
        pads_made = sem("pads_made")
        dve_step = sem("dve_step")
        coef_made = sem("coef_made")
        vec_rows_turned = sem("vec_rows_turned")
        vec_made = sem("vec_made")
        l0_step = sem("l0_step")
        act_step = sem("act_step")
        lhs_cols = sem("lhs_cols")
        a_hi = sem("a_hi")
        a_made = sem("a_made")
        lhs_built = sem("lhs_built")
        quad_made = sem("quad_made")
        transposed = sem("transposed")
        hi_made = sem("hi_made")
        lo_made = sem("lo_made")
        pre_made = sem("pre_made")
        tanh_made = sem("tanh_made")
        main_made = sem("main_made")
        x3_made = sem("x3_made")
        score_made = sem("score_made")
        piece_made = sem("piece_made")
        piece_hi = sem("piece_hi")
        piece_dve = sem("piece_dve")
        piece_act = sem("piece_act")
        g_split = sem("g_split")
        soft_pe = sem("soft_pe")
        soft_dve = sem("soft_dve")
        e_made = sem("e_made")
        e_split = sem("e_split")
        ew_made = sem("ew_made")
        nm_made = sem("nm_made")
        arg_made = sem("arg_made")
        exp_made = sem("exp_made")
        e_spread = sem("e_spread")
        zb_hi = sem("zb_hi")
        zb_made = sem("zb_made")
        z_made = sem("z_made")
        rz_made = sem("rz_made")
        wt_hi = sem("wt_hi")
        wt_lo = sem("wt_lo")
        xh_made = sem("xh_made")
        xl_dve = sem("xl_dve")
        xl_pool = sem("xl_pool")
        sums_made = sem("sums_made")
        cs_hi = sem("cs_hi")
        cs_made = sem("cs_made")
        pooled = sem("pooled")
        out_act = sem("out_act")
        out_dve = sem("out_dve")
        out_pool = sem("out_pool")

        N_VEC = BATCH + 2
        N_WLOAD = 7
        PIECES = 13
        BY_ACT = (6, 7, 8, 9, 10, 12)

        def count_of(mine, upto):
            return sum(1 for m in range(upto + 1) if mine(m))

        def read_by_act(k):
            return k % PIECES in BY_ACT

        def wait_piece_read(eng, k):
            if read_by_act(k):
                eng.wait_ge(piece_act, count_of(read_by_act, k))
            else:
                eng.wait_ge(piece_dve, count_of(lambda m: not read_by_act(m), k))

        def wait_x3(eng, blk):
            eng.wait_ge(x3_made, blk + 1)

        def low_by_pool(blk):
            return blk in POOL_LOWS

        def wait_low(eng, blk):
            if low_by_pool(blk):
                eng.wait_ge(xl_pool, count_of(low_by_pool, blk))
            else:
                eng.wait_ge(xl_dve, count_of(lambda m: not low_by_pool(m), blk))

        def shared_end(blk):
            return blk in SHARED_ENDS

        def wait_bank_taken(eng, blk):
            if shared_end(blk):
                eng.wait_ge(out_act, count_of(shared_end, blk))
            else:
                eng.wait_ge(out_dve, count_of(lambda m: not shared_end(m), blk))

        def wait_out(eng, blk):
            if shared_end(blk):
                eng.wait_ge(out_pool, count_of(shared_end, blk))
            else:
                eng.wait_ge(out_dve, count_of(lambda m: not shared_end(m), blk))

        def y_loads(n):
            g = n % GROUPS
            return (3 if g == 0 else 1) + (3 if g == GROUPS - 1 else 1) + 1

        def y_count(n):
            return 16 * sum(y_loads(m) for m in range(n % 2, n + 1, 2))

        def wait_low_buffer(eng, blk):
            b, q = divmod(blk, NBLK)
            if b:
                eng.wait_ge(pooled, NBLK * (b - 1) + q + 1)
            elif q < 4:
                eng.wait_ge(transposed, KC * NG)
            elif q < 12:
                eng.wait_ge(main_made, T * (NG - 1))
            else:
                eng.wait_ge(main_made, T * NG)

        def low_part(eng, blk):
            q = blk % NBLK
            wait_low_buffer(eng, blk)
            eng.wait_ge(xh_made, blk + 1)
            return eng.tensor_tensor(xl[q], x3[:, blk, :], xh[:, q, :].bitcast(F32), ALU.subtract)

        def turn_at(n):
            return {2: (0, 1), 3: (2, 3)} if n == 0 else {1: (0, 1), 2: (2, 3)}

        def max_bank(b, j):
            return [misc, tr_ps[1]][j % 2]

        block = ctx.enter_context(nc.Block())

        @block.sync
        def _(sp):
            def load_group(n):
                b, g = divmod(n, GROUPS)
                r0 = g * ROWS
                t, s = y[n % 2], y_loaded[n % 2]
                if n >= 2:
                    sp.wait_ge(l0_step, 10 * (n - 1))
                sp.dma_start(t[:, 1:T + 1, 1:D + 1],
                             x[b, r0:r0 + ROWS, :].rearrange("(p t) d -> p t d", t=T)).then_inc(s, 16)
                if g == 0:
                    sp.dma_start(t[0:1, 0, 1:D + 1], x[b, 1:2, :]).then_inc(s, 16)
                    sp.dma_start(t[1:16, 0, 1:D + 1],
                                 x[b, T - 1:T - 1 + 15 * T, :].rearrange("(p t) d -> p t d", t=T)[:, 0, :]
                                 ).then_inc(s, 16)
                    sp.dma_start(t[16:P, 0, 1:D + 1],
                                 x[b, 16 * T - 1:ROWS - 1, :].rearrange("(p t) d -> p t d", t=T)[:, 0, :]
                                 ).then_inc(s, 16)
                else:
                    sp.dma_start(t[:, 0, 1:D + 1],
                                 x[b, r0 - 1:r0 - 1 + ROWS, :].rearrange("(p t) d -> p t d", t=T)[:, 0, :]
                                 ).then_inc(s, 16)
                if g == GROUPS - 1:
                    sp.dma_start(t[P - 1:P, T + 1, 1:D + 1], x[b, S - 2:S - 1, :]).then_inc(s, 16)
                    sp.dma_start(t[P - 16:P - 1, T + 1, 1:D + 1],
                                 x[b, S - 16 * T + T:S, :].rearrange("(p t) d -> p t d", t=T)[:, 0, :]
                                 ).then_inc(s, 16)
                    sp.dma_start(t[0:P - 16, T + 1, 1:D + 1],
                                 x[b, r0 + T:r0 + T + (P - 16) * T, :].rearrange("(p t) d -> p t d", t=T)[:, 0, :]
                                 ).then_inc(s, 16)
                else:
                    sp.dma_start(t[:, T + 1, 1:D + 1],
                                 x[b, r0 + T:r0 + T + ROWS, :].rearrange("(p t) d -> p t d", t=T)[:, 0, :]
                                 ).then_inc(s, 16)

            def load_weights(b):
                cat = sp.value_load(idx[0:1, b:b + 1], min_val=0, max_val=cat_w.shape[0] - 1)
                lang = sp.value_load(idx[0:1, BATCH + b:BATCH + b + 1], min_val=0, max_val=lora_a.shape[0] - 1)
                if b:
                    wait_piece_read(sp, PIECES * (b - 1) + 9)
                    sp.wait_ge(g_split, (KC + 1) * b)
                sp.dma_start(wg, cat_w[bass.ds(cat, 1)].rearrange("a (c p) o -> p (a c) o", p=P)
                             ).then_inc(w_loaded[b], 16)
                sp.dma_start(b_raw[b], lora_b[bass.ds(lang, 1)].rearrange("a (c p) r -> p (a c) r", p=P)
                             ).then_inc(w_loaded[b], 16)
                if b == 0:
                    sp.wait_ge(zeroed, 1)
                for i in range(4):
                    sp.dma_start(a_raw[b][32 * i:32 * i + RANK, :],
                                 lora_a[bass.ds(lang, 1)].rearrange("a r d -> (a r) d")
                                 ).then_inc(w_loaded[b], 16)
                sp.dma_start(b_bc[b], cat_b[bass.ds(cat, 1)].to_broadcast([P, D])).then_inc(w_loaded[b], 16)

            def load_embed(b):
                lang = sp.value_load(idx[0:1, BATCH + b:BATCH + b + 1], min_val=0, max_val=lora_a.shape[0] - 1)
                sp.dma_start(vec_rows[b * KC:(b + 1) * KC, :],
                             lang_embed[bass.ds(lang, 1)].rearrange("a (c p) -> (a c) p", p=P)
                             ).then_inc(vec_loaded, 16)

            sp.dma_start(idx[0:1, 0:BATCH], cat_ids.rearrange("(a n) -> a n", a=1)).then_inc(idx_loaded, 16)
            sp.dma_start(idx[0:1, BATCH:2 * BATCH], lang_ids.rearrange("(a n) -> a n", a=1)).then_inc(idx_loaded, 16)
            load_group(0)
            sp.wait_ge(idx_loaded, 32)
            for b in range(BATCH):
                load_embed(b)
            load_weights(0)
            sp.dma_start(pid_i[:], prompt_ids.rearrange("(a n) -> a n", a=1).to_broadcast([P, BATCH])
                         ).then_inc(small_loaded, 16)
            sp.dma_start(w1_sb[:], w1.rearrange("(c p) a -> p c a", p=P)).then_inc(small_loaded, 16)
            for n in range(1, 4):
                load_group(n)
            load_weights(1)
            for n in range(4, NG):
                load_group(n)

        @block.gpsimd
        def _(pool):
            steps = [0]

            def step(ins):
                steps[0] += 1
                ins.then_inc(pool_step, 1)

            def link(ins):
                step(ins)
                pool.wait_ge(pool_step, steps[0])

            for b in range(BATCH):
                step(pool.memset(l1w[b], 0.0))
                step(pool.memset(a_raw[b], 0.0))
            pool.wait_ge(pool_step, steps[0])
            pool.memset(ident[:], 0.0).then_inc(zeroed, 1)
            step(pool.memset(sel_f, 0.0))
            pool.wait_ge(zeroed, 1)
            link(pool.affine_select(out=ident[:], in_=ident[:], compare_op=ALU.not_equal, fill=1.0,
                                    base=0, pattern=[[-1, P]], channel_multiplier=1))
            for i, at_row in ((0, RANK), (0, 64 + RANK), (1, 0), (1, 32)):
                link(pool.affine_select(out=sel_f[:, i, :], in_=sel_f[:, i, :], compare_op=ALU.not_equal, fill=1.0,
                                        base=-at_row, pattern=[[0, P]], channel_multiplier=1))
            step(pool.memset(ones_r[:].bitcast(F32), 1.0))
            link(pool.memset(ones[:], 1.0))
            pool.engine_nop().then_inc(consts_made, 1)

            def pads(n):
                pool.wait_ge(y_loaded[n % 2], y_count(n))
                pool.tensor_copy(y[n % 2][:, 1:T + 1, 0:D + 2:D + 1],
                                 y[n % 2][:, 1:T + 1, 2:D:D - 3]).then_inc(pads_made, 1)

            pads(0)
            step(pool.memset(below, 0.0))
            step(pool.memset(above, 0.0))
            step(pool.memset(rep[:], 0.0))
            step(pool.memset(ew[:].bitcast(F32), 0.0))
            step(pool.memset(e_quad[:], 0.0))
            pool.wait_ge(pool_step, steps[0])
            step(pool.affine_select(out=below, in_=below, compare_op=ALU.is_ge, fill=1.0,
                                    base=0, pattern=[[-1, P]], channel_multiplier=1))
            step(pool.affine_select(out=above, in_=above, compare_op=ALU.is_ge, fill=1.0,
                                    base=0, pattern=[[1, P]], channel_multiplier=-1))
            pads(1)
            step(pool.affine_select(out=rep[:].rearrange("q (a m) -> q a m", m=NBLK),
                                    in_=rep[:].rearrange("q (a m) -> q a m", m=NBLK),
                                    compare_op=ALU.not_equal, fill=1.0,
                                    base=0, pattern=[[0, P // NBLK], [-1, NBLK]], channel_multiplier=1))
            link(pool.iota(row_no[:], [[P, NBLK]], base=1, channel_multiplier=1))
            link(pool.tensor_copy(row_nof[:], row_no[:]))
            pool.wait_ge(small_loaded, 32)
            link(pool.tensor_copy(pidf[:], pid_i[:]))
            link(pool.tensor_scalar(kind[:, 0, :], pidf[:], 0.0, None, ALU.is_equal))
            link(pool.tensor_scalar(kind[:, 1, :], pidf[:], 1.0, None, ALU.is_equal))
            link(pool.tensor_tensor(kind[:, 2, :], kind[:, 0, :], kind[:, 1, :], ALU.add))
            link(pool.tensor_scalar(kind[:, 2, :], kind[:, 2, :], -1.0, 1.0, ALU.mult, ALU.add))
            link(pool.tensor_scalar(pen[:, 0, :], kind[:, 1, :], NEG, None, ALU.mult))
            link(pool.tensor_scalar(pen[:, 1, :], kind[:, 2, :], NEG, None, ALU.mult))
            link(pool.tensor_scalar(pen[:, 2, :], kind[:, 0, :], NEG, None, ALU.mult))
            link(pool.tensor_tensor(count_ab[:, 0, :], kind[:, 0, :], kind[:, 1, :], ALU.subtract))
            link(pool.tensor_scalar(count_ab[:, 1, :], kind[:, 1, :], float(S + 1), None, ALU.mult))
            link(pool.tensor_scalar(count_ab[:, 2, :], kind[:, 2, :], float(S - 1), None, ALU.mult))
            link(pool.tensor_tensor(count_ab[:, 1, :], count_ab[:, 1, :], count_ab[:, 2, :], ALU.add))
            n = NBLK
            for b in range(BATCH):
                link(pool.tensor_scalar(count[:, b, :], row_nof[:], count_ab[:, 0, b:b + 1], count_ab[:, 1, b:b + 1],
                                        ALU.mult, ALU.add))
                for m, parts, w in ((mask[:, b, :], ((below, 0), (ident, 1), (above, 2)), P),
                                    (bm[:, b, :], ((below, 0), (ident, NEG), (above, 2)), n),
                                    (bmt[:, b, :], ((below, 2), (ident, NEG), (above, 0)), n)):
                    for i, (c, by) in enumerate(parts):
                        by = by if by == NEG else pen[0:w, by, b:b + 1]
                        d = m if i == 0 else pool_tmp[0:w, 0:w]
                        link(pool.tensor_scalar(d, c[0:w, 0:w], by, None, ALU.mult))
                        if i:
                            link(pool.tensor_tensor(m, m, d, ALU.add))
                pads(2 + b)
            pool.engine_nop().then_inc(masks_made, 1)

            for n in range(2 + BATCH, NG):
                pads(n)

            def weights_of_sums(b):
                pool.wait_ge(e_split, b + 1)
                if b:
                    pool.wait_ge(sums_made, b)
                for i in range(4):
                    pool.tensor_copy(ew[:, 32 * i::P + 1], e_hi[:].bitcast(F32)).then_inc(ew_made, 1)
                    pool.tensor_copy(ew[:, 32 * i + NBLK::P + 1], e_lo[:].bitcast(F32)).then_inc(ew_made, 1)

            def end_block(blk):
                if shared_end(blk):
                    pool.wait_ge(out_act, count_of(shared_end, blk))
                    pool.tensor_tensor(ot[blk % 4], ot[blk % 4], x3[:, blk, :], ALU.add).then_inc(out_pool, 1)

            weights_of_sums(0)
            for q in range(NBLK):
                end_block(q)
                if q and low_by_pool(NBLK + q - 1):
                    low_part(pool, NBLK + q - 1).then_inc(xl_pool, 1)
                if q == 8:
                    weights_of_sums(1)
            if low_by_pool(2 * NBLK - 1):
                low_part(pool, 2 * NBLK - 1).then_inc(xl_pool, 1)
            for q in range(NBLK, 2 * NBLK):
                end_block(q)
        @block.scalar
        def _(act):
            for i, src in enumerate((z_x, z_y, z_r)):
                act.dma_start(zs[:, i, :], src.rearrange("(a n) -> a n", a=1).to_broadcast([P, BATCH])
                              ).then_inc(zs_loaded, 16)
            for i, src in enumerate((b1, v)):
                act.dma_start(vec_rows[BATCH * KC + i:BATCH * KC + i + 1, :], src.rearrange("(a n) -> a n", a=1)
                              ).then_inc(vec_loaded, 16)

            def make_quad(n, h):
                b = n // GROUPS
                if n == 0 and h == 0:
                    act.wait_ge(coef_made, 1)
                act.wait_ge(pads_made, n + 1)
                if n:
                    act.wait_ge(l0_step, 10 * (n - 1) + 5 * (h + 1))
                act.activation(quad[h][:], y[n % 2][:, 1 + NHALF * h:1 + NHALF * (h + 1), 1:D + 1],
                               ACT.Identity, bias=coef[:, 1, b:b + 1], scale=coef[:, 0, b:b + 1]
                               ).then_inc(quad_made, 1)

            def split_hi(n, c):
                act.wait_ge(transposed, KC * n + c + 1)
                if n >= 2:
                    act.wait_ge(main_made, T * (n - 1))
                act.activation(xt_hi[n % 2][:, c, :], tr_ps[c % 2][:], ACT.Copy).then_inc(hi_made, 1)

            def build_cols(b):
                act.wait_ge(w_loaded[b], 16 * N_WLOAD)
                for i in range(4):
                    act.activation(l1w[b][:, :, 32 * i:32 * i + RANK], b_raw[b], ACT.Copy).then_inc(lhs_cols, 1)
                act.wait_ge(vec_made, 1)
                for i in (0, 2):
                    act.activation(l1w[b][:, :, 32 * i + RANK:32 * i + RANK + 1],
                                   vec[:, KC * b:KC * (b + 1)].rearrange("p (c o) -> p c o", o=1), ACT.Copy
                                   ).then_inc(lhs_cols, 1)
                if b:
                    act.wait_ge(piece_made, PIECES * (b - 1) + 6)
                act.activation(a_st[:], a_raw[b], ACT.Copy).then_inc(a_hi, 1)

            def piece(b, i):
                src = piece_bank(b, i)
                k = PIECES * b + i
                if i == 0:
                    act.wait_ge(piece_made, k + 1)
                    if b:
                        act.wait_ge(piece_made, PIECES * (b - 1) + 6)
                    act.activation(b_st[:], src[:], ACT.Copy).then_inc(piece_hi, 1)
                elif i == 1:
                    wait_piece_read(act, k)
                    act.activation(c_st[b][:], cbias[b][0:64, :], ACT.Copy).then_inc(piece_hi, 1)
                elif i < 6:
                    wait_piece_read(act, k)
                    act.activation(g_hi[b][:, i - 2, :], wg[:, i - 2, :], ACT.Copy).then_inc(piece_hi, 1)
                elif i < 10:
                    act.wait_ge(piece_made, k + 1)
                    if b and i == 6:
                        act.wait_ge(piece_made, PIECES * (b - 1) + 12)
                    act.activation(gt[:, i - 6, :], src[:], ACT.Copy).then_inc(piece_act, 1)
                elif i == 10:
                    act.wait_ge(piece_made, k + 1)
                    act.activation(ct[:], src[:, 0:KC], ACT.Copy).then_inc(piece_act, 1)
                elif i == 11:
                    act.wait_ge(piece_made, k + 1)
                    act.activation(gw_hi[b][:].rearrange("p c a -> p (c a)"), src[:], ACT.Copy).then_inc(piece_hi, 1)
                else:
                    act.wait_ge(piece_made, k + 1)
                    act.activation(pbias[:, b:b + 1], src[:, 0:1], ACT.Identity,
                                   bias=vec[:, BATCH * KC:BATCH * KC + 1]).then_inc(piece_act, 1)

            def tanh(n):
                b = n // GROUPS
                act.wait_ge(pre_made, n + 1)
                if n % GROUPS == 0:
                    wait_piece_read(act, PIECES * (b + 1) - 1)
                if n:
                    act.wait_ge(score_made, n)
                act.activation(h_t[:], pre_ps[:], ACT.Tanh, bias=pbias[:, b:b + 1]).then_inc(tanh_made, 1)

            def take_block(blk):
                act.wait_ge(main_made, blk + 1)
                if blk == 15:
                    wait_piece_read(act, 2 * PIECES - 3)
                if blk == 16:
                    wait_piece_read(act, 2 * PIECES - 1)
                    act.wait_ge(masks_made, 1)
                act.activation(x3[:, blk, :], main_ps[blk % 3][:], ACT.Copy).then_inc(x3_made, 1)

            def high_part(blk):
                q = blk % NBLK
                if blk == 0:
                    act.wait_ge(l0_step, 10 * NG)
                if blk >= NBLK:
                    act.wait_ge(pooled, blk - NBLK + 1)
                wait_x3(act, blk)
                act.activation(xh[:, q, :], x3[:, blk, :], ACT.Copy).then_inc(xh_made, 1)

            def soft_exp(b):
                act.wait_ge(soft_dve, 3 * b + 3)
                act.activation(e_f[:], esub[:], ACT.Exp).then_inc(e_made, 1)

            def zb_parts(b):
                act.wait_ge(soft_pe, 3 * b + 3)
                act.activation(zb[:, b, :], misc[:, 0:2], ACT.Copy).then_inc(zb_hi, 1)

            def chunk_exp(b, j):
                act.wait_ge(arg_made, 4 * b + j + 1)
                for i in (1, 0):
                    t = pu[:, j % 2, i, :, :]
                    act.activation(t, t, ACT.Exp).then_inc(exp_made, 1)
                if b and j == 0:
                    act.wait_ge(main_made, T * NG)
                c = slice(4 * j, 4 * j + 4)
                act.wait_ge(exp_made, 8 * b + 2 * j + 1)
                act.activation(us[b][:, c, :], pu[:, j % 2, 1, :, :], ACT.Copy).then_inc(wt_hi, 1)
                act.wait_ge(exp_made, 8 * b + 2 * j + 2)
                act.activation(ph[b][:, c, :], pu[:, j % 2, 0, :, :], ACT.Copy).then_inc(wt_hi, 1)

            def sums_hi(b):
                act.wait_ge(sums_made, b + 1)
                if b:
                    act.wait_ge(pooled, NBLK * b)
                act.activation(cs[:], sum_ps[:], ACT.Copy).then_inc(cs_hi, 1)

            def end_block(blk):
                if not shared_end(blk):
                    return
                b, q = divmod(blk, NBLK)
                act.wait_ge(pooled, blk + 1)
                act.wait_ge(rz_made, blk // 4 + 1)
                if blk >= 4:
                    act.wait_ge(out_stored[blk % 4], 16 * (blk // 4))
                act.activation(ot[blk % 4], out_ps[blk % 4][:], ACT.Copy, scale=rz[:, b, q:q + 1]
                               ).then_inc(out_act, 1)

            make_quad(0, 0)
            make_quad(0, 1)
            build_cols(0)
            make_quad(1, 0)
            piece(0, 0)
            for c in range(2):
                split_hi(0, c)
            for i in range(1, 6):
                piece(0, i)
                if i == 2:
                    for c in range(2, 4):
                        split_hi(0, c)
            make_quad(1, 1)
            highs_due = []
            for n in range(NG):
                for k in range(T):
                    if k == 0 and n:
                        tanh(n)
                    if n == 6 and k == 0:
                        zb_parts(0)
                    take_block(T * n + k)
                    if n == 0:
                        for i in LEAD_PIECES[k]:
                            piece(0, i)
                    if n + 1 < NG and k in turn_at(n):
                        for c in turn_at(n)[k]:
                            split_hi(n + 1, c)
                    for i in highs_due:
                        piece(1, i)
                    highs_due = []
                    if 1 <= n < 4:
                        for i in NEXT_PIECES[n - 1][k]:
                            if 1 <= i < 6:
                                highs_due.append(i)
                            else:
                                piece(1, i)
                    if k == 0 and 1 <= n < NG - 2:
                        make_quad(n + 2, 1)
                    if n == 5 and k == 0:
                        soft_exp(0)
                    if n == 0 and k in (2, 3):
                        make_quad(2, k - 2)
                    if k == T - 1 and 1 <= n < NG - 3:
                        make_quad(n + 3, 0)
                    if n >= NG - 2:
                        for q in range(2):
                            high_part(2 * (T * (n - NG + 2) + k) + q)
                    if (n, k) in EXP_AT:
                        chunk_exp(0, EXP_AT[(n, k)])
                if n == 0:
                    tanh(0)
                    build_cols(1)
                    make_quad(3, 0)

            sums_hi(0)
            soft_exp(1)
            for q in range(NBLK):
                end_block(q)
                if q == 2:
                    zb_parts(1)
                if q >= 1:
                    high_part(NBLK + q - 1)
                if q in (7, 11):
                    chunk_exp(1, q // 4 - 1)
            high_part(2 * NBLK - 1)
            sums_hi(1)
            chunk_exp(1, 2)
            for q in range(NBLK, 2 * NBLK):
                if q == NBLK + 2:
                    chunk_exp(1, 3)
                end_block(q)

        @block.tensor
        def _(pe):
            def piece(b, i, n=0):
                k = PIECES * b + i
                o = piece_bank(b, i)
                if i:
                    wait_piece_read(pe, PIECES * b + READS_PIECE[i])
                if b and i in IN_PRE_BANK:
                    pe.wait_ge(tanh_made, n + 1)
                before = [m for m in range(k) if piece_bank(*divmod(m, PIECES)) is o]
                if before:
                    wait_piece_read(pe, before[-1])
                if i == 0:
                    pe.wait_ge(lhs_cols, 6 * (b + 1))
                    pe.wait_ge(lhs_built, b + 1)
                    for c in range(KC):
                        m = pe.matmul(o[:], l1w[b][:, c, :], wg[:, c, :], start=(c == 0), stop=(c == KC - 1))
                elif i == 1:
                    m = pe.matmul(o[:], sel[:, 0, :], b_st[:], start=True, stop=True)
                elif i < 6:
                    c = i - 2
                    if c == 0:
                        pe.wait_ge(a_made, b + 1)
                    m = pe.matmul(o[:], a_st[:, c * P:(c + 1) * P], b_st[:], start=True, stop=True)
                elif i < 10:
                    mc = i - 6
                    for c in range(KC):
                        m = pe.transpose(o[:, c * P:(c + 1) * P], wg[:, c, mc * P:(mc + 1) * P], ident[:])
                elif i == 10:
                    for c in range(KC):
                        m = pe.matmul(o[:, c:c + 1], cbias[b][0:1, c * P:(c + 1) * P], ones[0:1, 0:1],
                                      start=True, stop=True)
                elif i == 11:
                    pe.wait_ge(small_loaded, 32)
                    for c in range(KC):
                        for mc in range(KC):
                            m = pe.matmul(o[:, c * P:(c + 1) * P], gt[:, mc, c * P:(c + 1) * P],
                                          w1_sb[:, mc, :], start=(mc == 0), stop=(mc == KC - 1))
                else:
                    for mc in range(KC):
                        m = pe.matmul(o[:, 0:1], w1_sb[:, mc, :], ct[:, mc:mc + 1],
                                      start=(mc == 0), stop=(mc == KC - 1))
                m.then_inc(piece_made, 1)

            def turn_chunk(n, c):
                if c == 0:
                    pe.wait_ge(l0_step, 10 * (n + 1))
                k = KC * n + c
                if k >= 2:
                    pe.wait_ge(lo_made, k - 1)
                rows = tr_ps[c % 2][:].rearrange("d (p t) -> d t p", t=T)
                for t in range(T):
                    m = pe.transpose(rows[:, t, :], x1[t // NHALF][:, t % NHALF, c * P:(c + 1) * P], ident[:])
                m.then_inc(transposed, 1)

            def three(out, hi, lo, r_hi, r_lo, first, last):
                pe.matmul(out, hi, r_hi, start=first, stop=False)
                pe.matmul(out, hi, r_lo, start=False, stop=False)
                return pe.matmul(out, lo, r_hi, start=False, stop=last)

            def pre_group(n):
                b, i = n // GROUPS, n % 2
                if n % GROUPS == 0:
                    wait_piece_read(pe, PIECES * b + 11)
                    wait_piece_read(pe, PIECES * b + 12)
                pe.wait_ge(lo_made, KC * (n + 1))
                if n:
                    pe.wait_ge(tanh_made, n)
                in_bank = [i for i in IN_PRE_BANK if 2 <= n <= 4 and i <= LAST_PIECE[n - 2]]
                if in_bank:
                    wait_piece_read(pe, PIECES + in_bank[-1])
                for c in range(KC):
                    m = three(pre_ps[:], gw_hi[b][:, c, :], gw_lo[b][:, c, :], xt_hi[i][:, c, :], xt_lo[i][:, c, :],
                              c == 0, c == KC - 1)
                m.then_inc(pre_made, 1)

            def main_block(n, k):
                b, i, blk = n // GROUPS, n % 2, T * n + k
                if k == 0:
                    pe.wait_ge(lo_made, KC * (n + 1))
                    if n % GROUPS == 0:
                        pe.wait_ge(g_split, (KC + 1) * (b + 1) if n else 1)
                if blk >= 3:
                    wait_x3(pe, blk - 3)
                rows = slice(k * P, (k + 1) * P)
                pe.matmul(main_ps[blk % 3][:], sel[0:64, 1, :], c_st[b][:], start=True, stop=False)
                for c in range(KC):
                    if blk == 0:
                        pe.wait_ge(g_split, 2 + c)
                    m = three(main_ps[blk % 3][:], xt_hi[i][:, c, rows], xt_lo[i][:, c, rows],
                              g_hi[b][:, c, :], g_lo[b][:, c, :], False, c == KC - 1)
                m.then_inc(main_made, 1)

            def score_rows(n, half):
                pe.wait_ge(tanh_made, n + 1)
                if n == GROUPS:
                    pe.wait_ge(soft_dve, 1)
                for k in (2 * half, 2 * half + 1):
                    m = pe.matmul(sc_ps[:, T * n + k:T * n + k + 1], h_t[:, k * P:(k + 1) * P],
                                  vec[:, BATCH * KC + 1:BATCH * KC + 2], start=True, stop=True)
                if half:
                    m.then_inc(score_made, 1)

            def soft_turn(b):
                pe.wait_ge(soft_dve, 3 * b + 1)
                if b:
                    pe.wait_ge(arg_made, 4 * b)
                pe.transpose(misc[0:NBLK, 0:P], sc[:, b, :], ident[:]).then_inc(soft_pe, 1)

            def soft_spread(b):
                pe.wait_ge(soft_dve, 3 * b + 2)
                pe.matmul(misc[:, 0:NBLK], ones[0:NBLK, :], diagb[:], start=True, stop=True)
                pe.matmul(misc[:, NBLK:2 * NBLK], rep[:], xb16[:], start=True, stop=True).then_inc(soft_pe, 1)

            def soft_zb(b):
                pe.wait_ge(e_spread, b + 1)
                pe.wait_ge(soft_dve, 3 * b + 3)
                pe.matmul(misc[:, 0:2], e_quad[:], ones[:, 0:2], start=True, stop=True).then_inc(soft_pe, 1)

            def chunk_max(b, j):
                if j == 0:
                    pe.wait_ge(soft_dve, 3 * b + 3)
                    pe.wait_ge(zb_made, b + 1)
                if j == 1 and b == 0:
                    pe.wait_ge(lo_made, KC * NG)
                if 4 * b + j >= 2:
                    pe.wait_ge(arg_made, 4 * b + j - 1)
                for k in range(4):
                    q = 4 * j + k
                    m = pe.matmul(max_bank(b, j)[:, k * P:(k + 1) * P],
                                  pick[:, q:q + 1].to_broadcast([32 + NBLK, P]), nm_st[:], start=True, stop=True)
                m.then_inc(nm_made, 1)

            def chunk_sum(b, j):
                k = 4 * b + j
                pe.wait_ge(wt_lo, 2 * (k + 1))
                if j == 0:
                    pe.wait_ge(zb_made, b + 1)
                if k:
                    pe.wait_ge(rz_made, k)
                for q in range(4 * j, 4 * j + 4):
                    o = z_ps[:, 2 * q:2 * q + 2]
                    pe.matmul(o, ph[b][:, q, :], ones_r[:], start=True, stop=False)
                    pe.matmul(o, pl[b][:, q, :], ones_r[:], start=False, stop=False)
                    m = pe.matmul(o, us[b][:, q, :], zb[:, b, :], start=False, stop=True)
                m.then_inc(z_made, 1)

            def sums(b, q):
                if q == 0:
                    pe.wait_ge(ew_made, 8 * (b + 1))
                    if b == 0:
                        pe.wait_ge(tanh_made, NG)
                    else:
                        pe.wait_ge(cs_made, b)
                wait_low(pe, NBLK * b + q)
                lhs = ew[:, q * P:(q + 1) * P]
                pe.matmul(sum_ps[:], lhs, xh[:, q, :], start=(q == 0), stop=False)
                m = pe.matmul(sum_ps[:], lhs, xl[q], start=False, stop=(q == NBLK - 1))
                if q == NBLK - 1:
                    m.then_inc(sums_made, 1)

            def pool_own(b, q):
                blk = NBLK * b + q
                if blk < 3:
                    wait_x3(pe, BATCH * NBLK - 3 + (blk + 1) % 3)
                elif blk == 3:
                    pe.wait_ge(soft_dve, 4)
                else:
                    wait_bank_taken(pe, blk - 4)
                o = out_ps[blk % 4][:]
                pe.matmul(o, ph[b][:, q, :], xh[:, q, :], start=True, stop=False)
                pe.matmul(o, ph[b][:, q, :], xl[q], start=False, stop=False)
                pe.matmul(o, pl[b][:, q, :], xh[:, q, :], start=False, stop=False)

            def pool_others(b, q):
                if q == 0:
                    pe.wait_ge(cs_made, b + 1)
                pe.matmul(out_ps[(NBLK * b + q) % 4][:], us[b][:, q, :], cs[:], start=False, stop=True
                          ).then_inc(pooled, 1)

            def pool_blocks(b, between):
                chunk_sum(b, 0)
                for q in range(4):
                    pool_own(b, q)
                for q in range(4):
                    pool_others(b, q)
                between(3)
                for q in range(4, NBLK):
                    if q % 4 == 0:
                        chunk_sum(b, q // 4)
                    pool_own(b, q)
                    pool_others(b, q)
                    between(q)

            pe.wait_ge(consts_made, 1)
            pe.wait_ge(vec_loaded, 16 * N_VEC)
            pe.transpose(tr_ps[0][:, 0:BATCH * KC + 2], vec_rows, ident[0:BATCH * KC + 2, 0:BATCH * KC + 2]
                         ).then_inc(vec_rows_turned, 1)
            pe.wait_ge(vec_made, 1)
            piece(0, 0)
            turn_chunk(0, 0)
            turn_chunk(0, 1)
            for i in range(1, 4):
                piece(0, i)
            turn_chunk(0, 2)
            turn_chunk(0, 3)
            for i in range(4, 6):
                piece(0, i)
            for n in range(NG):
                if n:
                    pre_group(n)
                for k in range(T):
                    main_block(n, k)
                    if n == 0:
                        for i in LEAD_PIECES[k]:
                            piece(0, i)
                    if n + 1 < NG and k in turn_at(n):
                        for c in turn_at(n)[k]:
                            turn_chunk(n + 1, c)
                    if 1 <= n < 4:
                        for i in NEXT_PIECES[n - 1][k]:
                            piece(1, i, n)
                    if n == 1 and k == 0:
                        for half in range(2):
                            score_rows(0, half)
                    if n and k in (1, 2):
                        score_rows(n, k - 1)
                    if (n, k) == (4, 0):
                        soft_turn(0)
                    if (n, k) == (4, 2):
                        soft_spread(0)
                    if (n, k) == (5, 3):
                        soft_zb(0)
                    if (n, k) in MAX_AT:
                        chunk_max(0, MAX_AT[(n, k)])
                if n == 0:
                    pre_group(0)

            for q in range(NBLK):
                sums(0, q)
                if q == 3:
                    soft_turn(1)
                if q == 11:
                    soft_spread(1)

            def between(q):
                if q == 3:
                    soft_zb(1)
                if q in (5, 9, 13):
                    chunk_max(1, q // 4 - 1)

            pool_blocks(0, between)
            for q in range(NBLK):
                sums(1, q)
                if q == 3:
                    chunk_max(1, 3)
            pool_blocks(1, lambda q: None)

        @block.vector
        def _(dve):
            chain = [0]

            def link(ins):
                chain[0] += 1
                ins.then_inc(dve_step, 1)
                dve.wait_ge(dve_step, chain[0])

            def build_lhs(b):
                dve.wait_ge(w_loaded[b], 16 * N_WLOAD)
                for c in range(KC):
                    d = wg[:, c, c * P:(c + 1) * P]
                    m = dve.tensor_tensor(d, d, ident[:], ALU.add)
                m.then_inc(lhs_built, 1)

            def split_a(b):
                dve.wait_ge(a_hi, b + 1)
                for i in (32, 96):
                    m = dve.tensor_tensor(a_st[i:i + 32, :], a_raw[b][i:i + 32, :], a_st[i:i + 32, :].bitcast(F32),
                                          ALU.subtract)
                m.then_inc(a_made, 1)

            def piece(b, i):
                k = PIECES * b + i
                src = piece_bank(b, i)
                if read_by_act(k):
                    return
                dve.wait_ge(piece_made, k + 1)
                if i == 0:
                    dve.wait_ge(piece_hi, 7 * b + 1)
                    m = dve.tensor_tensor(b_st[64:P, :], src[64:P, :], b_st[64:P, :].bitcast(F32), ALU.subtract)
                elif i == 1:
                    m = dve.tensor_tensor(cbias[b], src[:], b_bc[b], ALU.add)
                elif i < 6:
                    m = dve.tensor_tensor(wg[:, i - 2, :], src[:], wg[:, i - 2, :], ALU.add)
                elif i == 11:
                    dve.wait_ge(piece_hi, 7 * b + 7)
                    m = dve.tensor_tensor(gw_lo[b][:].rearrange("p c a -> p (c a)"), src[:],
                                          gw_hi[b][:].rearrange("p c a -> p (c a)").bitcast(F32), ALU.subtract)
                m.then_inc(piece_dve, 1)

            def piece_low(b, i):
                dve.wait_ge(piece_hi, 7 * b + i + 1)
                if i == 1:
                    dve.tensor_tensor(c_st[b][32:64, :], cbias[b][32:64, :], c_st[b][32:64, :].bitcast(F32),
                                      ALU.subtract).then_inc(g_split, 1)
                else:
                    dve.tensor_tensor(g_lo[b][:, i - 2, :], wg[:, i - 2, :], g_hi[b][:, i - 2, :].bitcast(F32),
                                      ALU.subtract).then_inc(g_split, 1)

            def stencil(n, h, o):
                b = n // GROUPS
                t = y[n % 2]
                r = 1 + NHALF * h
                k = 10 * n + 5 * h
                if k + o:
                    dve.wait_ge(l0_step, k + o)
                if o == 0:
                    dve.wait_ge(pads_made, n + 1)
                    m = dve.tensor_tensor(lap[:], t[:, r:r + NHALF, 0:D], t[:, r:r + NHALF, 2:D + 2], ALU.add)
                elif o == 1:
                    dve.wait_ge(quad_made, 2 * n + h + 1)
                    m = dve.tensor_tensor(quad[h][:], quad[h][:], t[:, r:r + NHALF, 1:D + 1], ALU.mult)
                elif o == 2:
                    m = dve.scalar_tensor_tensor(lap[:], lap[:], zs[:, 0, b:b + 1], quad[h][:], ALU.mult, ALU.add)
                elif o == 3:
                    m = dve.tensor_tensor(quad[h][:], t[:, r - 1:r - 1 + NHALF, 1:D + 1],
                                          t[:, r + 1:r + 1 + NHALF, 1:D + 1], ALU.add)
                else:
                    if n:
                        dve.wait_ge(transposed, KC * n)
                    m = dve.scalar_tensor_tensor(x1[h][:], quad[h][:], zs[:, 1, b:b + 1], lap[:], ALU.mult, ALU.add)
                m.then_inc(l0_step, 1)

            def split_lo(n, c):
                dve.wait_ge(hi_made, KC * n + c + 1)
                if n >= 2:
                    dve.wait_ge(main_made, T * (n - 1))
                dve.tensor_tensor(xt_lo[n % 2][:, c, :], tr_ps[c % 2][:], xt_hi[n % 2][:, c, :].bitcast(F32),
                                  ALU.subtract).then_inc(lo_made, 1)

            def soft_take(b):
                dve.wait_ge(score_made, GROUPS * (b + 1))
                dve.tensor_copy(sc[:, b, :], sc_ps[:, b * NBLK:(b + 1) * NBLK]).then_inc(soft_dve, 1)

            def soft_scan(b):
                dve.wait_ge(soft_pe, 3 * b + 1)
                if b == 0:
                    dve.wait_ge(masks_made, 1)
                    link(dve.memset(sfx[:, P:P + 1], NEG))
                    link(dve.memset(nm_st[:].bitcast(F32), 0.0))
                link(dve.memset(pmx[:, 0:1], NEG))
                link(dve.tensor_copy(s16[:], misc[0:NBLK, 0:P]))
                dve.tensor_tensor_scan(sfx[:, P - 1::-1], s16[:, P - 1::-1], s16[:, P - 1::-1], NEG,
                                       ALU.max, ALU.max).then_inc(dve_step, 1)
                chain[0] += 1
                link(dve.tensor_tensor_scan(pmx[:, 1:P + 1], s16[:], s16[:], NEG, ALU.max, ALU.max))
                dve.tensor_scalar(diagb[:], ident[0:NBLK, 0:NBLK], pmx[:, P:P + 1], None, ALU.mult
                                  ).then_inc(dve_step, 1)
                chain[0] += 1
                dve.wait_ge(dve_step, chain[0])
                dve.tensor_scalar(xb16[:], bm[:, b, :], pmx[:, P:P + 1], None, ALU.add).then_inc(soft_dve, 1)

            def soft_max(b):
                dve.wait_ge(soft_pe, 3 * b + 2)
                link(dve.tensor_tensor(esub[:], sc[:, b, :], misc[:, 0:NBLK], ALU.subtract))
                link(dve.tensor_copy(bmb[:], misc[:, NBLK:2 * NBLK]))
                link(dve.tensor_tensor(tmp16[:], misc[0:NBLK, 0:NBLK], bmt[:, b, :], ALU.add))
                link(dve.reduce_max(be[:], tmp16[:], AX_X))
                mrow = pmx[:, 0:P]
                link(dve.tensor_scalar(mrow, mrow, pen[0:NBLK, 0, b:b + 1], be[:], ALU.add, ALU.max))
                link(dve.scalar_tensor_tensor(mrow, sfx[:, 1:P + 1], pen[0:NBLK, 2, b:b + 1], mrow,
                                              ALU.add, ALU.max))
                link(dve.scalar_tensor_tensor(mrow, s16[:], pen[0:NBLK, 1, b:b + 1], mrow, ALU.add, ALU.max))
                if b:
                    dve.wait_ge(nm_made, 4 * b)
                link(dve.tensor_scalar(nm_st[0:NBLK, :], mrow, -1.0, None, ALU.mult))
                dve.scalar_tensor_tensor(nm_st[32:32 + NBLK, :], mrow, -1.0, nm_st[0:NBLK, :].bitcast(F32),
                                         ALU.mult, ALU.subtract).then_inc(soft_dve, 1)

            def soft_split(b):
                dve.wait_ge(e_made, b + 1)
                if b:
                    dve.wait_ge(soft_pe, 3 * b)
                dve.tensor_copy(e_quad[:].rearrange("p (g m) -> p g m", g=4)[:, :, 0:NBLK],
                                e_f[:].rearrange("p (o m) -> p o m", o=1).to_broadcast([P, 4, NBLK])
                                ).then_inc(e_spread, 1)
                if b:
                    dve.wait_ge(ew_made, 8 * b)
                link(dve.tensor_copy(e_hi[:], e_f[:]))
                dve.tensor_tensor(e_lo[:], e_f[:], e_hi[:].bitcast(F32), ALU.subtract).then_inc(e_split, 1)

            def zb_lows(b):
                dve.wait_ge(zb_hi, b + 1)
                for i in (32, 96):
                    m = dve.tensor_tensor(zb[i:i + 32, b, :], misc[i:i + 32, 0:2], zb[i:i + 32, b, :].bitcast(F32),
                                          ALU.subtract)
                m.then_inc(zb_made, 1)

            def chunk_args(b, j):
                dve.wait_ge(nm_made, 4 * b + j + 1)
                k = 4 * b + j
                if k >= 2:
                    dve.wait_ge(wt_lo, 2 * (k - 1))
                p = pu[:, j % 2, 0, :, :]
                for i in range(4):
                    dve.scalar_tensor_tensor(p[:, i, :], max_bank(b, j)[:, i * P:(i + 1) * P],
                                             sc[:, b, 4 * j + i:4 * j + i + 1], mask[:, b, :], ALU.add, ALU.add)
                dve.tensor_tensor(pu[:, j % 2, 1, :, :], max_bank(b, j)[:].rearrange("p (q i) -> p q i", q=4),
                                  bmb[:, 4 * j:4 * j + 4].rearrange("p (q o) -> p q o", o=1).to_broadcast([P, 4, P]),
                                  ALU.add).then_inc(arg_made, 1)

            def chunk_rz(b, j):
                dve.wait_ge(z_made, 4 * b + j + 1)
                c = slice(4 * j, 4 * j + 4)
                link(dve.tensor_tensor(zc[:, c], z_ps[:, 8 * j:8 * j + 8:2], count[:, b, c], ALU.mult))
                dve.reciprocal(rz[:, b, c], zc[:, c]).then_inc(rz_made, 1)

            def chunk_lo(b, j):
                c = slice(4 * j, 4 * j + 4)
                dve.wait_ge(wt_hi, 2 * (4 * b + j) + 2)
                dve.tensor_tensor(us[b][64:P, c, :], pu[64:P, j % 2, 1, :, :], us[b][64:P, c, :].bitcast(F32),
                                  ALU.subtract).then_inc(wt_lo, 1)
                dve.tensor_tensor(pl[b][:, c, :], pu[:, j % 2, 0, :, :], ph[b][:, c, :].bitcast(F32), ALU.subtract
                                  ).then_inc(wt_lo, 1)

            def sums_lo(b):
                dve.wait_ge(cs_hi, b + 1)
                for s in (32, 96):
                    m = dve.tensor_tensor(cs[s:s + 32, :], sum_ps[s:s + 32, :], cs[s:s + 32, :].bitcast(F32),
                                          ALU.subtract)
                m.then_inc(cs_made, 1)

            def end_block(blk):
                b, q = divmod(blk, NBLK)
                if q % 4 == 0:
                    chunk_rz(b, q // 4)
                if shared_end(blk):
                    return
                dve.wait_ge(pooled, blk + 1)
                dve.wait_ge(rz_made, blk // 4 + 1)
                if blk >= 4:
                    dve.wait_ge(out_stored[blk % 4], 16 * (blk // 4))
                dve.scalar_tensor_tensor(ot[blk % 4], out_ps[blk % 4][:], rz[:, b, q:q + 1], x3[:, blk, :],
                                         ALU.mult, ALU.add).then_inc(out_dve, 1)

            def low(blk):
                if not low_by_pool(blk):
                    low_part(dve, blk).then_inc(xl_dve, 1)

            dve.wait_ge(zs_loaded, 48)
            link(dve.tensor_scalar(coef[:, 0, :], zs[:, 2, :], -1.0, None, ALU.mult))
            link(dve.tensor_tensor(z_sum[:], zs[:, 0, :], zs[:, 1, :], ALU.add))
            link(dve.tensor_scalar(z_sum[:], z_sum[:], -2.0, 1.0, ALU.mult, ALU.add))
            dve.tensor_tensor(coef[:, 1, :], z_sum[:], zs[:, 2, :], ALU.add).then_inc(coef_made, 1)
            dve.wait_ge(consts_made, 1)
            link(dve.tensor_copy(sel[:], sel_f))
            link(dve.memset(pick[:].bitcast(F32), 0.0))
            link(dve.tensor_copy(pick[0:NBLK, :], ident[0:NBLK, 0:NBLK]))
            link(dve.tensor_copy(pick[32:32 + NBLK, :], ident[32:32 + NBLK, 32:32 + NBLK]))
            for o in range(4):
                stencil(0, 0, o)
            dve.wait_ge(vec_rows_turned, 1)
            dve.tensor_copy(vec[:], tr_ps[0][:, 0:BATCH * KC + 2]).then_inc(vec_made, 1)
            stencil(0, 0, 4)
            build_lhs(0)
            for o in range(4):
                stencil(0, 1, o)
            split_a(0)
            stencil(0, 1, 4)
            piece(0, 0)
            for c in range(2):
                split_lo(0, c)
            piece(0, 1)
            for i in range(2, 6):
                piece(0, i)
                piece_low(0, i - 1)
                if i == 3:
                    for c in range(2, 4):
                        split_lo(0, c)
            piece_low(0, 5)
            for h in range(2):
                for o in range(5):
                    stencil(1, h, o)
            lows_due = [[], []]
            for n in range(NG):
                ops = [(h, o) for h in range(2) for o in range(5)] if n + 2 < NG else []
                for k in range(T):
                    if n == 0:
                        for i in LEAD_PIECES[k]:
                            piece(0, i)
                    if 1 <= n < 4:
                        for i in lows_due[0]:
                            piece_low(1, i)
                        lows_due = [lows_due[1], [i for i in NEXT_PIECES[n - 1][k] if 1 <= i < 6]]
                    first = STEPS_BEFORE[n][k]
                    then = 3 if n and k == 2 else 0
                    for o in ops[:first]:
                        stencil(n + 2, *o)
                    if n + 1 < NG and k in turn_at(n):
                        for c in turn_at(n)[k]:
                            split_lo(n + 1, c)
                    for o in ops[first:first + then]:
                        stencil(n + 2, *o)
                    ops = ops[first + then:]
                    if 1 <= n < 4:
                        for i in NEXT_PIECES[n - 1][k]:
                            piece(1, i)
                    if (n, k) == (3, 3):
                        soft_take(0)
                    if (n, k) == (4, 1):
                        soft_scan(0)
                    if (n, k) == (4, 3):
                        soft_max(0)
                    if (n, k) == (5, 1):
                        soft_split(0)
                    if (n, k) == (6, 0):
                        zb_lows(0)
                    if (n, k) == (7, 3):
                        soft_take(1)
                    if (n, k) in LO_AT:
                        chunk_lo(0, LO_AT[(n, k)])
                    if (n, k) in ARGS_AT:
                        chunk_args(0, ARGS_AT[(n, k)])
                    for q in ROWS_LO_AT.get((n, k), ()):
                        low(q)
                if n == 0:
                    for o in ops:
                        stencil(2, *o)
                    build_lhs(1)
                    split_a(1)

            soft_scan(1)
            for q in range(12, NBLK):
                low(q)
            soft_max(1)
            sums_lo(0)
            soft_split(1)
            for q in range(NBLK):
                end_block(q)
                if q == 2:
                    zb_lows(1)
                if q:
                    low(NBLK + q - 1)
                if q in (5, 9):
                    chunk_args(1, q // 4 - 1)
                if q in (8, 12):
                    chunk_lo(1, q // 4 - 2)
            low(2 * NBLK - 1)
            chunk_args(1, 2)
            sums_lo(1)
            for q in range(NBLK, 2 * NBLK):
                end_block(q)
                if q == NBLK:
                    chunk_args(1, 3)
                if q in (NBLK + 2, NBLK + 5):
                    chunk_lo(1, 2 + (q - NBLK) // 5)

        @block.sync
        def _(sp):
            for blk in range(BATCH * NBLK):
                b, q = divmod(blk, NBLK)
                wait_out(sp, blk)
                sp.dma_start(out[b, q * P:(q + 1) * P, :], ot[blk % 4]).then_inc(out_stored[blk % 4], 16)
            for i in range(4):
                sp.wait_ge(out_stored[i], 16 * (BATCH * NBLK // 4))


STEPS_BEFORE = [(0, 0, 0, 2), (2, 0, 0, 5), (3, 1, 0, 3), (3, 1, 0, 3), (4, 0, 0, 3), (3, 0, 0, 4), (0,) * 4, (0,) * 4]
POOL_LOWS = tuple(range(17, 30, 2))
SHARED_ENDS = (2, 6, 9, 12, 15, 16, 19, 22, 25, 28)
LEAD_PIECES = [(6, 7), (8, 9), (10, 11), (12,)]
NEXT_PIECES = [[(), (), (0,), (1,)], [(2,), (3, 4), (5,), ()], [(6, 7), (8, 9), (10, 11), (12,)]]
LAST_PIECE = [max(sum(group, ())) for group in NEXT_PIECES]
IN_PRE_BANK = (4, 9, 11)
READS_PIECE = {1: 0, 2: 0, 3: 0, 4: 0, 5: 0, 6: 5, 7: 5, 8: 5, 9: 5, 10: 1, 11: 9, 12: 10}
MAX_AT = {(6, 1): 0, (6, 3): 1, (7, 0): 2, (7, 1): 3}
ARGS_AT = {(6, 1): 0, (6, 3): 1, (7, 0): 2, (7, 1): 3}
EXP_AT = {(6, 2): 0, (6, 3): 1, (7, 1): 2, (7, 2): 3}
LO_AT = {(6, 3): 0, (7, 0): 1, (7, 2): 2, (7, 3): 3}
ROWS_LO_AT = {(6, 3): (0, 1, 2, 3), (7, 0): (4, 5), (7, 1): (6, 7, 8), (7, 2): (9, 10, 11)}

_INS = ["x", "condB_zX", "condB_zY", "condB_zR", "itok_B_0_3", "itok_B_0_30", "itok_B_0_2", "L1_cond_lora_A",
        "L1_cond_lora_B", "L1_cond_lang_embed", "L2_cond_W", "L2_cond_b", "L3_cond_W1", "L3_cond_b1", "L3_cond_v"]


def kernel(**inputs):
    import concourse.bacc as bacc
    from concourse.bass_utils import run_bass_kernel_spmd

    nc = bacc.Bacc("TRN2", target_bir_lowering=False, num_devices=1, dynamic_dma_scratch_size=1024)
    arrays, args = {}, []
    for name in _INS:
        a = np.ascontiguousarray(inputs[name])
        arrays[f"in_{name}"] = a
        args.append(nc.dram_tensor(f"in_{name}", a.shape, mybir.dt.from_np(a.dtype), kind="ExternalInput").ap())
    shape = tuple(inputs["x"].shape)
    args.append(nc.dram_tensor("out", shape, F32, kind="ExternalOutput").ap())
    fused_layers(nc, *args)
    r = run_bass_kernel_spmd(nc, [arrays], core_ids=[0])
    return r.results[0]["out"]
```
